# Optimizing a Trainium2 kernel written in Bass

```python
import numpy as np
import jax
import jax.numpy as jnp

def _softmax(x, axis=-1):
    return jax.nn.softmax(x, axis=axis)

def _gelu(x):
    return jax.nn.gelu(x, approximate=True)

def _silu(x):
    return jax.nn.silu(x)

def _sigmoid(x):
    return jax.nn.sigmoid(x)

def _layernorm(x, axis=-1, eps=1e-05):
    m = jnp.mean(x, axis=axis, keepdims=True)
    v = jnp.var(x, axis=axis, keepdims=True)
    return (x - m) / jnp.sqrt(v + eps)

def _scatter_add(tgt, idx, src, axis=0):
    return tgt.at[idx].add(src)

def _segment_sum(src, seg, n):
    return jax.ops.segment_sum(src, seg, n)
kernel_name = 'mk_seq_postln_d2_jaxref_r8_804cb2'

def setup_inputs(seed: int=0):
    np.random.seed(seed)
    _w = jnp.asarray

    def _L0_attn_setup():
        import jax, jax.numpy as jnp
        import numpy as np
        DIM = 256
        HEADS = 16
        B = 2
        T = 256
        key = jax.random.key(seed)
        k_x, k_qkv, k_out, k_b = jax.random.split(key, 4)
        inv = DIM ** (-0.5)
        return {'x': jax.random.normal(k_x, (B, T, DIM), dtype=jnp.float32), 'w_qkv': jax.random.normal(k_qkv, (DIM, 3 * DIM), dtype=jnp.float32) * inv, 'w_out': jax.random.normal(k_out, (DIM, DIM), dtype=jnp.float32) * inv, 'b_out': jnp.zeros((DIM,), dtype=jnp.float32)}
    _L0_attn_in = _L0_attn_setup()

    def _L0_ffn_setup():
        import jax, jax.numpy as jnp
        import numpy as np
        D_MODEL = 256
        D_EXPERT = 1024
        EPS = 1e-08

        def ternary_quant(w):
            scale = jnp.mean(jnp.abs(w)) + EPS
            q = jnp.clip(jnp.round(w / scale), -1.0, 1.0) * scale
            return w + jax.lax.stop_gradient(q - w)
        key = jax.random.key(seed)
        k_x, k_up, k_gate, k_down = jax.random.split(key, 4)
        std_in = 1.0 / np.sqrt(D_MODEL)
        std_exp = 1.0 / np.sqrt(D_EXPERT)
        return {'x': jax.random.normal(k_x, (4, 256, D_MODEL), dtype=jnp.float32), 'W_up': jax.random.normal(k_up, (D_EXPERT, D_MODEL), dtype=jnp.float32) * std_in, 'W_gate': jax.random.normal(k_gate, (D_EXPERT, D_MODEL), dtype=jnp.float32) * std_in, 'W_down': jax.random.normal(k_down, (D_MODEL, D_EXPERT), dtype=jnp.float32) * std_exp}
    _L0_ffn_in = _L0_ffn_setup()

    def _L1_attn_setup():
        import jax, jax.numpy as jnp
        import numpy as np
        DIM = 256
        N_HEADS = 16
        N_KV_HEADS = 4
        WINDOW = 64
        GLOBAL = 64

        def alibi_slopes(num_heads):
            closest_pow2 = 2.0 ** np.floor(np.log2(num_heads))
            base = 2.0 ** (-2.0 ** (-(np.log2(closest_pow2) - 3.0)))
            powers = np.arange(1, 1 + num_heads, dtype=np.float32)
            return jnp.asarray(base ** powers, dtype=jnp.float32)

        def window_allowed(seq_len):
            i = jnp.arange(seq_len)[:, None]
            j = jnp.arange(seq_len)[None, :]
            inside = (j >= i - WINDOW // 2) & (j <= i + WINDOW // 2)
            glob = (i < GLOBAL) | (j < GLOBAL)
            return inside | glob
        key = jax.random.key(seed)
        k1, k2, k3, k4 = jax.random.split(key, 4)
        B, S, D = (2, 256, DIM)
        kv_feat = 2 * D * N_KV_HEADS // N_HEADS
        std = 0.02
        x = jax.random.normal(k1, (B, S, D), dtype=jnp.float32)
        Wq = jax.random.normal(k2, (D, D), dtype=jnp.float32) * std
        Wkv = jax.random.normal(k3, (D, kv_feat), dtype=jnp.float32) * std
        Wo = jax.random.normal(k4, (D, D), dtype=jnp.float32) * std
        bo = jnp.zeros((D,), dtype=jnp.float32)
        return {'x': x, 'Wq': Wq, 'Wkv': Wkv, 'Wo': Wo, 'bo': bo}
    _L1_attn_in = _L1_attn_setup()

    def _L1_ffn_setup():
        import jax, jax.numpy as jnp
        import numpy as np
        DIM_IN = 256
        DIM_HIDDEN = 1024
        key = jax.random.key(seed)
        k_x, k_g, k_u, k_d = jax.random.split(key, 4)
        s_in = 1.0 / np.sqrt(DIM_IN)
        s_hid = 1.0 / np.sqrt(DIM_HIDDEN)
        x = jax.random.normal(k_x, (4, 256, DIM_IN), dtype=jnp.float32)
        w_gate = jax.random.uniform(k_g, (DIM_HIDDEN, DIM_IN), jnp.float32, -s_in, s_in)
        w_up = jax.random.uniform(k_u, (DIM_HIDDEN, DIM_IN), jnp.float32, -s_in, s_in)
        w_down = jax.random.uniform(k_d, (DIM_IN, DIM_HIDDEN), jnp.float32, -s_hid, s_hid)
        return {'x': x, 'w_gate': w_gate, 'w_up': w_up, 'w_down': w_down}
    _L1_ffn_in = _L1_ffn_setup()
    _d = {'L0_attn_x': _L0_attn_in['x'], 'L0_attn_w_qkv': _L0_attn_in['w_qkv'], 'L0_attn_w_out': _L0_attn_in['w_out'], 'L0_attn_b_out': _L0_attn_in['b_out'], 'L0_ffn_W_up': _L0_ffn_in['W_up'], 'L0_ffn_W_gate': _L0_ffn_in['W_gate'], 'L0_ffn_W_down': _L0_ffn_in['W_down'], 'L1_attn_Wq': _L1_attn_in['Wq'], 'L1_attn_Wkv': _L1_attn_in['Wkv'], 'L1_attn_Wo': _L1_attn_in['Wo'], 'L1_attn_bo': _L1_attn_in['bo'], 'L1_ffn_w_gate': _L1_ffn_in['w_gate'], 'L1_ffn_w_up': _L1_ffn_in['w_up'], 'L1_ffn_w_down': _L1_ffn_in['w_down']}
    _x0 = _d['L0_attn_x']
    _d['L0_attn_x'] = jax.random.normal(jax.random.fold_in(jax.random.key(seed), 1), (2, 1024, 256), dtype=_x0.dtype)
    del _x0
    return _d

def reference(L0_attn_x, L0_attn_w_qkv, L0_attn_w_out, L0_attn_b_out, L0_ffn_W_up, L0_ffn_W_gate, L0_ffn_W_down, L1_attn_Wq, L1_attn_Wkv, L1_attn_Wo, L1_attn_bo, L1_ffn_w_gate, L1_ffn_w_up, L1_ffn_w_down):

    def _L0_attn_ref(x, w_qkv, w_out, b_out):
        import jax, jax.numpy as jnp
        import numpy as np
        DIM = 256
        HEADS = 16
        B = 2
        T = 256
        b, t, e = x.shape
        h = HEADS
        d = e // h
        scale = d ** (-0.5)
        qkv = x @ w_qkv
        q, k, v = jnp.split(qkv, 3, axis=-1)
        q, k, v = (a.reshape(b, t, h, d).transpose(0, 2, 1, 3) for a in (q, k, v))
        dots = jnp.einsum('bhid,bhjd->bhij', q, k) * scale
        causal_mask = jnp.triu(jnp.ones((t, t), dtype=bool), k=1)
        dots = jnp.where(causal_mask[None, None, :, :], -jnp.inf, dots)
        attn = jax.nn.softmax(dots, axis=-1)
        out = jnp.einsum('bhij,bhjd->bhid', attn, v)
        out = out.transpose(0, 2, 1, 3).reshape(b, t, e)
        return out @ w_out + b_out

    def _L0_ffn_ref(x, W_up, W_gate, W_down):
        import jax, jax.numpy as jnp
        import numpy as np
        D_MODEL = 256
        D_EXPERT = 1024
        EPS = 1e-08

        def ternary_quant(w):
            scale = jnp.mean(jnp.abs(w)) + EPS
            q = jnp.clip(jnp.round(w / scale), -1.0, 1.0) * scale
            return w + jax.lax.stop_gradient(q - w)
        wu = ternary_quant(W_up)
        wg = ternary_quant(W_gate)
        wd = ternary_quant(W_down)
        up = jnp.einsum('bsd,ed->bse', x, wu)
        gate = jnp.einsum('bsd,ed->bse', x, wg)
        hidden = jax.nn.silu(up) * gate
        return jnp.einsum('bse,de->bsd', hidden, wd)

    def _L1_attn_ref(x, Wq, Wkv, Wo, bo):
        import jax, jax.numpy as jnp
        import numpy as np
        DIM = 256
        N_HEADS = 16
        N_KV_HEADS = 4
        WINDOW = 64
        GLOBAL = 64

        def alibi_slopes(num_heads):
            closest_pow2 = 2.0 ** np.floor(np.log2(num_heads))
            base = 2.0 ** (-2.0 ** (-(np.log2(closest_pow2) - 3.0)))
            powers = np.arange(1, 1 + num_heads, dtype=np.float32)
            return jnp.asarray(base ** powers, dtype=jnp.float32)

        def window_allowed(seq_len):
            i = jnp.arange(seq_len)[:, None]
            j = jnp.arange(seq_len)[None, :]
            inside = (j >= i - WINDOW // 2) & (j <= i + WINDOW // 2)
            glob = (i < GLOBAL) | (j < GLOBAL)
            return inside | glob
        B, S, D = x.shape
        H, KVH = (N_HEADS, N_KV_HEADS)
        hd = D // H
        r = H // KVH
        cw = jax.nn.sigmoid(jnp.sum(jnp.abs(x), axis=-1, keepdims=True))
        q = jnp.dot(x * cw, Wq)
        kv = jnp.dot(x, Wkv)
        k, v = jnp.split(kv, 2, axis=-1)
        q = q.reshape(B, S, H, hd).transpose(0, 2, 1, 3)
        k = k.reshape(B, S, KVH, hd).transpose(0, 2, 1, 3)
        v = v.reshape(B, S, KVH, hd).transpose(0, 2, 1, 3)
        k = jnp.repeat(k, r, axis=1)
        v = jnp.repeat(v, r, axis=1)
        scale = 1.0 / jnp.sqrt(jnp.float32(hd))
        qk = jnp.einsum('bhid,bhjd->bhij', q, k) * scale
        pos = jnp.arange(S)
        dist = -jnp.abs(pos[:, None] - pos[None, :]).astype(jnp.float32)
        qk = qk + alibi_slopes(H)[None, :, None, None] * dist[None, None, :, :]
        allowed = window_allowed(S)
        qk = jnp.where(allowed[None, None, :, :], -1000000000.0, qk)
        attn = jax.nn.softmax(qk, axis=-1)
        out = jnp.einsum('bhij,bhjd->bhid', attn, v)
        out = out.transpose(0, 2, 1, 3).reshape(B, S, D)
        return jnp.dot(out, Wo) + bo

    def _L1_ffn_ref(x, w_gate, w_up, w_down):
        import jax, jax.numpy as jnp
        import numpy as np
        DIM_IN = 256
        DIM_HIDDEN = 1024
        gate = jnp.einsum('bsd,hd->bsh', x, w_gate)
        up = jnp.einsum('bsd,hd->bsh', x, w_up)
        gated = jax.nn.silu(gate) * up
        return jnp.einsum('bsh,dh->bsd', gated, w_down)
    x = L0_attn_x
    x = _layernorm(x + _L0_attn_ref(x, L0_attn_w_qkv, L0_attn_w_out, L0_attn_b_out), axis=-1)
    x = _layernorm(x + _L0_ffn_ref(x, L0_ffn_W_up, L0_ffn_W_gate, L0_ffn_W_down), axis=-1)
    x = _layernorm(x + _L1_attn_ref(x, L1_attn_Wq, L1_attn_Wkv, L1_attn_Wo, L1_attn_bo), axis=-1)
    x = _layernorm(x + _L1_ffn_ref(x, L1_ffn_w_gate, L1_ffn_w_up, L1_ffn_w_down), axis=-1)
    return x

_drawn_inputs = setup_inputs


def setup_inputs(seed=0):
    import zlib

    import numpy as np

    out = dict(_drawn_inputs(seed))
    spreads = {'L0_attn_b_out': (0.0, 0.1), 'L1_attn_bo': (0.0, 0.1)}
    factors = {'L1_attn_Wq': 8.0, 'L1_attn_Wkv': 2.674}
    for name, (base, spread) in spreads.items():
        noise = np.random.default_rng([zlib.crc32(name.encode()), seed]).standard_normal(out[name].shape)
        drawn = base * np.exp(spread * noise) if base else spread * noise
        out[name] = jnp.asarray(drawn.astype(out[name].dtype))
    for name, factor in factors.items():
        out[name] = (out[name] * factor).astype(out[name].dtype)
    return out
```

```python
from contextlib import ExitStack

import numpy as np
import concourse.bass as bass
from concourse import mybir

ALU = mybir.AluOpType
ACT = mybir.ActivationFunctionType
AX = mybir.AxisListType
F32 = mybir.dt.float32
F32R = mybir.dt.float32r
BF16 = mybir.dt.bfloat16

P = 128
B, T, D = 2, 1024, 256
TOK = B * T
NT = TOK // P
TB = T // P
KD = D // P
H, HD = 16, 16
HG = 4
NG = H // HG
N = B * NG
E = 1024
KE = E // P
CH = 512
NC = TOK // CH
CT = CH // P
WIN, GLOB = 32, 64
PARTS = 3
Q_PART = (0, 0, 1, 1, 0, 2)
K_PART = (0, 1, 0, 1, 2, 0)
NPAIR = len(Q_PART)
NPOS = 9
LN_EPS = 1e-5
QUANT_EPS = 1e-8


class Chip:
    pass


class Dram:
    pass


class Layer:

    def __init__(self, index):
        self.index = index
        self.first_row = 0 if index == 0 else NPOS
        self.score_rows = self.first_row + NPAIR * HD
        self.rows = self.score_rows + 2
        self.key_sets = HG if index == 0 else 3
        self.kv_width = D if index == 0 else D // HG


def maximum_columns(layer, qt):
    return (0, (qt + 1) * P) if layer.index == 0 else (GLOB, T)


def cut(lo, hi):
    return [(a, min(b, hi)) for a, b in ((max(lo, c), c + CH) for c in range(0, T, CH)) if a < min(b, hi)]


def score_steps(qt):
    i0 = qt * P
    turn = max(GLOB, i0 + WIN)
    steps = [("left", a, b, 0) for a, b in cut(GLOB, turn)]
    steps += [("right", a, b, 0) for a, b in cut(turn, T)]
    steps += [("turn", a, b, 0) for a, b in cut(turn, i0 + 3 * WIN)]
    steps += [("band", a, b, a - (i0 - WIN)) for a, b in cut(max(GLOB, i0 - WIN), min(T, i0 + P + WIN))]
    return sorted(steps, key=lambda s: s[1] // CH)


def key_tile(layer, kt):
    if layer.index == 0:
        return kt * P, P
    j0 = GLOB + kt * P
    return j0, min(P, T - j0)


def columns_of(layer, half, kt):
    lo, hi = half * CH, (half + 1) * CH
    return (max(lo, kt * P), hi) if layer.index == 0 else (max(lo, GLOB), hi)


def quads_of(layer):
    return [(half, kt) for half in range(2) for kt in range(TB)
            if columns_of(layer, half, kt)[0] < columns_of(layer, half, kt)[1]]


def plan(layer, with_scores, with_values):
    quads = quads_of(layer) if with_values else []
    units = list(range(HG * TB)) if with_scores else []
    steps = []
    if not quads:
        return [("max", u) for u in units] + [("rows", 0)]
    last = len(quads) - 2
    given = 0
    for n, (half, kt) in enumerate(quads):
        due = min(len(units), -(-len(units) * (n + 1) // last)) if n < last else len(units)
        for h in range(HG):
            steps.append(("exp", HG * n + h))
            upto = given + (due - given) * (h + 1) // HG
            steps += [("max", u) for u in units[given:upto]] if h == HG - 1 else []
            if h < HG - 1:
                part = units[given:given + (due - given) // (HG - h)]
                steps += [("max", u) for u in part]
                given += len(part)
        given = due
        if n >= 1:
            steps.append(("values", n - 1))
            if quads[n - 1][0] != half:
                steps.append(("evict", quads[n - 1][0]))
        if n >= 2 and quads[n - 2][0] != quads[n - 1][0]:
            steps.append(("norm", quads[n - 2][0]))
        if units and n == last:
            steps.append(("rows", 0))
    steps += [("values", len(quads) - 1), ("evict", 1), ("norm", 1)]
    return steps


def project(nc, sem, sb, K, L, dram):
    i = L.index
    tag = str(i)
    ps, x, ident = K.ps, K.x, K.ident
    x_loaded = [sem(f"x_loaded{c}") for c in range(NC)] if i == 0 else None
    ident_loaded = sem("ident_loaded") if i == 0 else None
    const_loaded = sem("const_loaded") if i == 0 else None
    w_loaded = sem("wqkv_loaded" + tag)
    ffn_loaded = [sem(f"ffn_loaded{tag}{j}") for j in range(3)]
    xt_full = sem("xt_full" + tag)
    xt_act = sem("xt_act" + tag)
    xt_dve = sem("xt_dve" + tag)
    proj_full = sem("proj_full" + tag)
    part1 = sem("part1_done" + tag)
    rest1 = sem("rest1_done" + tag)
    part2 = sem("part2_done" + tag)
    part3 = sem("part3_done" + tag)
    sent = [sem(f"parts_sent{tag}{k}") for k in range(2)]
    v_full = sem("v_full" + tag)
    v_done = sem("v_done" + tag)
    cw_step = sem("cw_step" + tag)
    xc_ready = sem("xc_ready" + tag)
    ones_set = sem("ones_set" + tag)
    abs_sum = sem("abs_sum" + tag)
    total = sem("abs_total" + tag)
    tern = sem("ternary_step" + tag)
    w_hi = sem("w_hi" + tag)
    w_lo = sem("w_lo" + tag)

    NW = 3 * D if i == 0 else D + 2 * L.kv_width
    with ExitStack() as st:
        xt = sb(st, "xt" + tag, [P, KD, TOK], F32)
        w = sb(st, "wqkv" + tag, [P, KD, NW], F32)
        wf = sb(st, "wffn" + tag, [P, 3, KD * E], F32)
        part = sb(st, "part" + tag, [P, 2, PARTS, CH], BF16)
        rest = sb(st, "rest" + tag, [P, 2, CH], F32)
        if i == 0:
            wsum = sb(st, "wsum", [P, 3], F32)
            thr = sb(st, "thr", [P, 2, 3], F32)
            below = sb(st, "below", [P, KD * E], F32)
            units = [(b, m, c) for b in range(B) for m in range(2 * KD) for c in range(2)]
            v_units = [(b, c) for b in range(B) for c in range(TB // 2)]
        else:
            xct = sb(st, "xct", [P, KD, TOK], F32)
            xc = sb(st, "xc", [P, CT, D], F32)
            vt = sb(st, "vt", [P, B, T + GLOB], F32)
            cw = sb(st, "cw", [P, 4, NT], F32)
            units = [(b, m, c) for b in range(B) for m in (KD, 0, 1) for c in range(2)]
            v_units = list(range(B))
        turns = [(c, s, k) for c in range(NC) for s in range(1 + i) for k in range(KD)]

        def is_q(m):
            return m < KD

        def rows_of(m):
            return P if i == 0 or is_q(m) else L.kv_width

        block = st.enter_context(nc.Block())

        @block.sync
        def _(sp):
            if i == 0:
                xv = dram.x.rearrange("(t p) d -> p t d", p=P)
                sp.dma_start(ident[:], dram.ident).then_inc(ident_loaded, 16)
                for c in range(NC):
                    sp.dma_start(x[:, CT * c:CT * c + CT, :], xv[:, CT * c:CT * c + CT, :]).then_inc(x_loaded[c], 16)
            for u, (b, m, c) in enumerate(units):
                sp.wait_ge(part3, u + 1)
                sp.wait_ge(part2, u + 1)
                r = rows_of(m)
                dst = (dram.q_parts if is_q(m) else dram.k_parts)[i]
                row0 = (m % KD) * P
                dst = dst[:, b, row0:row0 + r, c * CH:(c + 1) * CH].rearrange("k r t -> r k t")
                sp.dma_start(dst, part[0:r, u % 2, :, :]).then_inc(sent[u % 2], 16)
            for k in range(2):
                sp.wait_ge(sent[k], 16 * (len(units) // 2))

        @block.gpsimd
        def _(pool):
            for j, wt in enumerate(dram.ffn[i]):
                wt = wt.rearrange("(k p) n -> p k n", p=P)
                pool.dma_start(wf[:, j, :].rearrange("p (k n) -> p k n", k=wt.shape[1]), wt).then_inc(ffn_loaded[j], 16)
            if i == 0:
                nc.gpsimd.memset(K.ones[:], 1.0).then_inc(ones_set, 1)
                nc.gpsimd.memset(K.power[:], -0.5).then_inc(ones_set, 1)
                pool.dma_start(K.identb[:], dram.identb).then_inc(const_loaded, 16)
                pool.dma_start(K.tri[:], dram.tri).then_inc(const_loaded, 16)
                pool.dma_start(K.band[:], dram.band).then_inc(const_loaded, 16)
                for j in range(2):
                    pool.dma_start(K.bias[:, j, :], dram.bias[j].to_broadcast((P, D))).then_inc(const_loaded, 16)
                pool.wait_ge(const_loaded, 16 * 5)
            else:
                for j in range(3):
                    pool.wait_ge(w_hi, j + 1)
                    nc.gpsimd.tensor_tensor(K.wffn[:, j, 1, :], wf[:, j, :], K.wffn[:, j, 0, :].bitcast(F32),
                                            ALU.subtract).then_inc(w_lo, 1)
                pool.wait_ge(w_lo, 3)

        @block.scalar
        def _(act):
            if i == 0:
                act.dma_start(w[:], dram.wq[0].rearrange("(k p) n -> p k n", p=P)).then_inc(w_loaded, 16)
            else:
                act.dma_start(w[:, :, 0:D], dram.wq[1].rearrange("(k p) n -> p k n", p=P)).then_inc(w_loaded, 16)
                act.dma_start(w[:, :, D:NW], dram.wkv.rearrange("(k p) n -> p k n", p=P)).then_inc(w_loaded, 16)
                act.wait_ge(cw_step, 1)
                nc.scalar.activation(cw[:, 1, :], cw[:, 0, :], ACT.Exp, scale=-1.0).then_inc(cw_step, 1)
            for n, (c, s, k) in enumerate(turns):
                if k == 0:
                    act.wait_ge(xt_full, n + 1)
                    dst = xct if s else xt
                    nc.scalar.copy(dst[:, k, c * CH:(c + 1) * CH], ps[:, n % 2, :]).then_inc(xt_act, 1)

            def second_part(u):
                r = rows_of(units[u][1])
                act.wait_ge(rest1, u + 1)
                nc.scalar.copy(part[0:r, u % 2, 1, :], rest[0:r, u % 2, :]).then_inc(part2, 1)

            for u, (b, m, c) in enumerate(units):
                r = rows_of(m)
                act.wait_ge(proj_full, u + 1)
                if u >= 2:
                    act.wait_ge(sent[u % 2], 16 * (u // 2))
                nc.scalar.activation(part[0:r, u % 2, 0, :], ps[0:r, 2 + u % 4, :], ACT.Copy,
                                     scale=0.25 if is_q(m) else 1.0).then_inc(part1, 1)
                if i == 1 and not is_q(m):
                    nc.scalar.copy(vt[r:P, b, c * CH:(c + 1) * CH], ps[r:P, 2 + u % 4, :]).then_inc(v_done, 1)
                    if c == 0:
                        nc.scalar.copy(vt[r:P, b, T:T + GLOB], ps[r:P, 2 + u % 4, 0:GLOB]).then_inc(v_done, 1)
                if u >= 1:
                    second_part(u - 1)
            second_part(len(units) - 1)
            for n, v in enumerate(v_units):
                act.wait_ge(v_full, n + 1)
                if i == 0:
                    b, c = v
                    for j in range(2):
                        nc.scalar.copy(K.v_all[:, b * NG:(b + 1) * NG, 2 * c + j, :],
                                       ps[:, 6 + n % 2, j * D:(j + 1) * D].rearrange("p (g d) -> p g d", g=NG)
                                       ).then_inc(v_done, 1)
                else:
                    nc.scalar.copy(K.v_all[:, v * NG:(v + 1) * NG, :, :],
                                   ps[:, 6 + v, :].rearrange("p (t g d) -> p g t d", t=TB, g=NG)).then_inc(v_done, 1)
            if i == 1:
                for j in range(3):
                    act.wait_ge(ffn_loaded[j], 16)
                    nc.scalar.copy(K.wffn[:, j, 0, :], wf[:, j, :]).then_inc(w_hi, 1)

        @block.vector
        def _(dve):
            if i == 1:
                nc.vector.tensor_reduce(cw[:, 0, :], x[:], AX.X, ALU.add,
                                        apply_absolute_value=True).then_inc(cw_step, 1)
                dve.wait_ge(cw_step, 2)
                nc.vector.tensor_scalar(cw[:, 2, :], cw[:, 1, :], 1.0, None, ALU.add).then_inc(cw_step, 1)
                dve.wait_ge(cw_step, 3)
                nc.vector.reciprocal(cw[:, 3, :], cw[:, 2, :]).then_inc(cw_step, 1)
                dve.wait_ge(cw_step, 4)

            def scaled(c):
                if c >= 1:
                    dve.wait_ge(xt_full, turns.index((c - 1, 1, 1)) + 1)
                for t in range(CT):
                    nc.vector.tensor_scalar(xc[:, t, :], x[:, CT * c + t, :], cw[:, 3, CT * c + t:CT * c + t + 1],
                                            None, ALU.mult).then_inc(xc_ready, 1)

            for n, (c, s, k) in enumerate(turns):
                if i == 1 and s == 0 and k == 0:
                    scaled(c)
                if k == 1:
                    dve.wait_ge(xt_full, n + 1)
                    dst = xct if s else xt
                    nc.vector.tensor_copy(dst[:, k, c * CH:(c + 1) * CH], ps[:, n % 2, :]).then_inc(xt_dve, 1)

            def third_part(u):
                r = rows_of(units[u][1])
                dve.wait_ge(part2, u + 1)
                nc.vector.tensor_tensor(part[0:r, u % 2, 2, :], rest[0:r, u % 2, :], part[0:r, u % 2, 1, :],
                                        ALU.subtract).then_inc(part3, 1)

            for u, (b, m, c) in enumerate(units):
                r = rows_of(m)
                dve.wait_ge(part1, u + 1)
                if u >= 2:
                    dve.wait_ge(part3, u - 1)
                nc.vector.scalar_tensor_tensor(
                    out=rest[0:r, u % 2, :], in0=ps[0:r, 2 + u % 4, :], scalar=0.25 if is_q(m) else 1.0,
                    in1=part[0:r, u % 2, 0, :], op0=ALU.mult, op1=ALU.subtract).then_inc(rest1, 1)
                if u >= 1:
                    third_part(u - 1)
            third_part(len(units) - 1)

            if i == 0:
                for j in range(3):
                    dve.wait_ge(ffn_loaded[j], 16)
                    nc.vector.tensor_reduce(wsum[:, j:j + 1], wf[:, j, :], AX.X, ALU.add,
                                            apply_absolute_value=True).then_inc(abs_sum, 1)
                dve.wait_ge(total, 1)
                nc.vector.tensor_scalar(K.scales[:], ps[:, 0, 0:3], 1.0 / (D * E), QUANT_EPS, ALU.mult,
                                        ALU.add).then_inc(tern, 1)
                dve.wait_ge(tern, 1)
                for s in range(2):
                    nc.vector.tensor_scalar(thr[:, s, :], K.scales[:], 0.5 - s, None, ALU.mult).then_inc(tern, 1)
                dve.wait_ge(tern, 3)
                for j in range(3):
                    if j >= 1:
                        dve.wait_ge(tern, 3 + 2 * j)
                    nc.vector.tensor_scalar(below[:], wf[:, j, :], thr[:, 1, j:j + 1], None, ALU.is_lt).then_inc(tern, 1)
                    dve.wait_ge(tern, 4 + 2 * j)
                    nc.vector.scalar_tensor_tensor(out=K.wffn[:, j, 0, :], in0=wf[:, j, :], scalar=thr[:, 0, j:j + 1],
                                                   in1=below[:], op0=ALU.is_gt, op1=ALU.subtract).then_inc(tern, 1)

        @block.tensor
        def _(pe):
            if i == 0:
                pe.wait_ge(ident_loaded, 16)
            for n, (c, s, k) in enumerate(turns):
                if i == 0 and k == 0:
                    pe.wait_ge(x_loaded[c], 16)
                if s == 1 and k == 0:
                    pe.wait_ge(xc_ready, CT * (c + 1))
                if n >= 2:
                    pe.wait_ge(xt_act if k == 0 else xt_dve, (n - 2) // 2 + 1)
                for j in range(CT):
                    src = xc[:, j, k * P:(k + 1) * P] if s else x[:, CT * c + j, k * P:(k + 1) * P]
                    last = nc.tensor.transpose(ps[:, n % 2, j * P:(j + 1) * P], src, ident[:])
                last.then_inc(xt_full, 1)
            pe.wait_ge(xt_act, len(turns) // 2)
            pe.wait_ge(xt_dve, len(turns) // 2)
            pe.wait_ge(w_loaded, 16 * (1 + i))
            for u, (b, m, c) in enumerate(units):
                if u >= 4:
                    pe.wait_ge(rest1, u - 3)
                    copies = sum((2 if cc == 0 else 1) for (_, mm, cc) in units[:u - 3] if mm == KD) if i else 0
                    if copies:
                        pe.wait_ge(v_done, copies)
                src = xct if i == 1 and is_q(m) else xt
                t0 = b * T + c * CH
                for k in range(KD):
                    last = nc.tensor.matmul(ps[:, 2 + u % 4, :], w[:, k, m * P:(m + 1) * P],
                                            src[:, k, t0:t0 + CH], start=(k == 0), stop=(k == KD - 1))
                last.then_inc(proj_full, 1)
            if i == 0:
                for n, (b, c) in enumerate(v_units):
                    if n >= 2:
                        pe.wait_ge(v_done, 2 * (n - 1))
                    for j in range(2):
                        t0 = b * T + (2 * c + j) * P
                        for k in range(KD):
                            last = nc.tensor.matmul(ps[:, 6 + n % 2, j * D:(j + 1) * D], xt[:, k, t0:t0 + P],
                                                    w[:, k, 2 * D:3 * D], start=(k == 0), stop=(k == KD - 1))
                    last.then_inc(v_full, 1)
                pe.wait_ge(abs_sum, 3)
                pe.wait_ge(ones_set, 1)
                nc.tensor.matmul(ps[:, 0, 0:3], K.ones[:], wsum[:], start=True, stop=True).then_inc(total, 1)
            else:
                pe.wait_ge(v_done, 3 * B)
                for b in v_units:
                    for t in range(TB):
                        j0 = GLOB + t * P
                        last = nc.tensor.transpose(ps[:, 6 + b, t * HG * HD:(t + 1) * HG * HD],
                                                   vt[L.kv_width:P, b, j0:j0 + P],
                                                   ident[L.kv_width:P, L.kv_width:P])
                    last.then_inc(v_full, 1)


def attend(nc, sem, sb, K, L, dram):
    i = L.index
    tag = str(i)
    ps, attn, ident, identb, tri, band = K.ps, K.attn, K.ident, K.identb, K.tri, K.band
    R0, RS, RA = L.first_row, L.score_rows, L.rows
    quads = quads_of(L)
    NU, NX, NQ = HG * TB, HG * len(quads), len(quads)
    last_quad = [max(q for q in range(NQ) if quads[q][0] == half) for half in range(2)]
    group_loads = NPAIR * (1 + (1 if i == 0 else L.key_sets)) + 2 * i
    S_BANK, T_BANK, O_BANK, SIDE = 0, 4, 6, 7
    loaded = [sem(f"operands_loaded{tag}{k}") for k in range(2)]
    fills = sem("constants_filled" + tag)
    FILLS = 2 + 2 * i
    const_rows = sem("constant_rows" + tag)
    v_staged = sem("v_staged" + tag)
    residual = sem("residual" + tag)
    s_full = sem("s_full" + tag)
    max_done = sem("max_done" + tag)
    m_high = sem("m_high" + tag)
    m_cut = sem("m_cut" + tag)
    m_turned = sem("m_turned" + tag)
    m_copied = sem("m_copied" + tag)
    m_sent = sem("m_sent" + tag)
    t_full = sem("t_full" + tag)
    exp_done = sem("exp_done" + tag)
    values_done = sem("values_done" + tag)
    evicted = sem("evicted" + tag)
    o_turned = sem("o_turned" + tag)
    o_rec = sem("o_rec" + tag)
    normed = sem("normed" + tag)
    with ExitStack() as st:
        qop = sb(st, "qop" + tag, [P, 2, HG, T], BF16)
        kop = sb(st, "kop" + tag, [P, 2, L.key_sets, T], BF16)
        turn = sb(st, "qturn", [P, 2, HG, T], BF16) if i == 1 else None
        v_heads = HG if i == 0 else 1
        vst = sb(st, "vst" + tag, [P, 2, TB + i, v_heads, 2 * HD], F32)
        prob = sb(st, "prob" + tag, [P, 2, HG, CH], F32)
        negm = sb(st, "negm" + tag, [P, 2, NU], F32)
        mpart = sb(st, "mpart" + tag, [P, 2, P // 2], BF16)
        mrow = sb(st, "mrow" + tag, [P, P], BF16)
        ot = sb(st, "ot" + tag, [P, CH], F32)
        rec = sb(st, "rec" + tag, [P, 2, CT * HG], F32)
        q_src = dram.q_parts[i].rearrange("k b (g h d) t -> k (b g) d h t", h=HG, d=HD)
        if i == 0:
            k_src = dram.k_parts[i].rearrange("k b (g h d) t -> k (b g) d h t", h=HG, d=HD)
        else:
            k_src = dram.k_parts[i].rearrange("k b (g d) t -> k (b g) d t", d=HD)
        first, steady, final = plan(L, True, False), plan(L, True, True), plan(L, False, True)
        block = st.enter_context(nc.Block())

        @block.sync
        def _(sp):
            def load(n, par):
                for r in range(NPAIR):
                    rows = slice(R0 + HD * r, R0 + HD * (r + 1))
                    sp.dma_start(qop[rows, par, :, :], q_src[Q_PART[r]][one(n)].rearrange("o d h t -> (o d) h t")).then_inc(loaded[par], 16)
                    if i == 0:
                        sp.dma_start(kop[rows, par, :, :],
                                     k_src[K_PART[r]][one(n)].rearrange("o d h t -> (o d) h t")).then_inc(loaded[par], 16)
                    else:
                        for v in range(L.key_sets):
                            sp.dma_start(kop[rows, par, v, :],
                                         k_src[K_PART[r]][one(n)].rearrange("o d t -> (o d) t")).then_inc(loaded[par], 16)
                if i == 1:
                    sp.dma_start(qop[0:NPOS, par, :, :], dram.qpos[one(n)].rearrange("o r h t -> (o r) h t")).then_inc(loaded[par], 16)
                    sp.dma_start(turn[0:NPOS, par, :, :], dram.qturn[one(n)].rearrange("o r h t -> (o r) h t")).then_inc(loaded[par], 16)

            def send_rows(n, par):
                sp.wait_ge(m_copied, n + 1)
                for k in range(2):
                    sp.dma_start(qop[RS + k:RS + k + 1, par, :, :].rearrange("o h t -> o (h t)"),
                                 mrow[k * P // 2:k * P // 2 + NU, :]).then_inc(m_sent, 16)

            for par in range(2):
                for v in range(L.key_sets):
                    sp.dma_start(kop[RS:RA, par, v, :], dram.kpos[NPOS - 2:NPOS, 0, :]).then_inc(const_rows, 16)
                    if i == 1:
                        sp.dma_start(kop[0:NPOS, par, v, :], dram.kpos[:, v, :]).then_inc(const_rows, 16)
            sp.wait_ge(fills, FILLS)
            load(0, 0)
            load(1, 1)
            send_rows(0, 0)
            with sp.Fori(0, N // 2 - 1) as pair:
                for par in range(2):
                    n = pair * 2 + par
                    send_rows(n + 1, 1 - par)
                    sp.wait_ge(values_done, (n + 1) * NQ)
                    load(n + 2, par)
            send_rows(N - 1, 1)

        @block.gpsimd
        def _(pool):
            nc.gpsimd.memset(vst[:], 1.0).then_inc(fills, 1)
            nc.gpsimd.memset(mpart[:], 0.0).then_inc(fills, 1)
            if i == 1:
                nc.gpsimd.memset(turn[:], 0.0).then_inc(fills, 1)
                pool.wait_ge(fills, 3)
                nc.gpsimd.memset(vst[GLOB:P, :, TB, :, :], 0.0).then_inc(fills, 1)
            pool.wait_ge(fills, FILLS)

            def stage(n, par):
                if i == 0:
                    nc.gpsimd.tensor_copy(vst[:, par, :, :, 0:HD],
                                          K.v_all[:, one(n), :, :].rearrange("p o t (h d) -> p (o t) h d", h=HG)
                                          ).then_inc(v_staged, 1)
                else:
                    nc.gpsimd.tensor_copy(vst[:, par, 0:TB, 0, 0:HD],
                                          K.v_all[:, one(n), :, :].rearrange("p o t d -> p (o t) d")
                                          ).then_inc(v_staged, 1)
                    nc.gpsimd.tensor_copy(vst[0:GLOB, par, TB:TB + 1, 0, 0:HD],
                                          K.v_all[0:GLOB, one(n), TB - 1:TB, :].rearrange("p o t d -> p (o t) d")
                                          ).then_inc(v_staged, 1)

            stage(0, 0)
            stage(1, 1)
            for t in range(NT):
                nc.gpsimd.tensor_tensor(K.x[:, t, :], K.x[:, t, :], K.bias[:, i, :], ALU.add).then_inc(residual, 1)
            pool.wait_ge(residual, NT)
            with pool.Fori(0, N // 2 - 1) as pair:
                for par in range(2):
                    n = pair * 2 + par
                    pool.wait_ge(values_done, (n + 1) * NQ)
                    stage(n + 2, par)

        def score_banks(u):
            return ps[:, S_BANK + 2 * (u % 2):S_BANK + 2 * (u % 2) + 2, :].rearrange("p a c -> p (a c)")

        @block.vector
        def _(dve):
            def step(pair, par, steps):
                n = pair * 2 + par
                for what, k in steps:
                    if what == "max":
                        lo, hi = maximum_columns(L, k % TB)
                        dve.wait_ge(s_full, (n + 1) * NU + k + 1)
                        nc.vector.tensor_reduce(negm[:, 1 - par, k:k + 1], score_banks(k)[:, lo:hi], AX.X, ALU.max,
                                                negate=True).then_inc(max_done, 1)
                    elif what == "rows":
                        dve.wait_ge(max_done, (n + 2) * NU)
                        nc.vector.tensor_copy(mpart[:, 0, 0:NU], negm[:, 1 - par, :]).then_inc(m_high, 1)
                        dve.wait_ge(m_high, n + 2)
                        nc.vector.tensor_tensor(mpart[:, 1, 0:NU], negm[:, 1 - par, :], mpart[:, 0, 0:NU],
                                                ALU.subtract).then_inc(m_cut, 1)
                        dve.wait_ge(m_turned, n + 2)
                        if steps is not first:
                            dve.wait_ge(m_sent, 32 * (n + 1))
                        nc.vector.tensor_copy(mrow[:], ps[:, SIDE, :].bitcast(BF16)[:, 0:P]
                                              ).then_inc(m_copied, 1)
                    elif what == "norm":
                        dve.wait_ge(o_turned, 2 * n + k + 1)
                        if k == 1:
                            dve.wait_ge(normed, 2 * n + 1)
                        side = ps[:, SIDE, :].rearrange("p (a d) -> p a d", d=2 * HD)
                        nc.vector.reciprocal(rec[:, k, :], side[:, :, HD]).then_inc(o_rec, 1)
                        dve.wait_ge(o_rec, 2 * n + k + 1)
                        nc.vector.tensor_tensor(
                            attn[:, one(pair), k * CT:(k + 1) * CT, par * HG * HD:(par + 1) * HG * HD]
                            .rearrange("p o t (h d) -> p (o t) h d", h=HG),
                            side[:, :, 0:HD].rearrange("p (t h) d -> p t h d", h=HG),
                            rec[:, k, :].rearrange("p (t h) -> p t h", h=HG).unsqueeze(3)
                            .to_broadcast((P, CT, HG, HD)), ALU.mult,
                        ).then_inc(normed, 1)

            step(-1, 1, first)
            with dve.Fori(0, N // 2 - 1) as pair:
                for par in range(2):
                    step(pair, par, steady)
            step(N // 2 - 1, 0, steady)
            step(N // 2 - 1, 1, final)

        @block.scalar
        def _(act):
            def step(n, par, steps):
                for what, k in steps:
                    if what == "exp":
                        half, kt = quads[k // HG]
                        lo, hi = columns_of(L, half, kt)
                        rows = key_tile(L, kt)[1]
                        q = k // HG
                        if k % HG == 0 and q >= 2:
                            act.wait_ge(values_done, n * NQ + q - 1)
                        act.wait_ge(t_full, n * NX + k + 1)
                        nc.scalar.activation(prob[0:rows, q % 2, k % HG, lo % CH:lo % CH + hi - lo],
                                             ps[0:rows, T_BANK + k % 2, lo % CH:lo % CH + hi - lo],
                                             ACT.Exp).then_inc(exp_done, 1)
                    elif what == "evict":
                        act.wait_ge(values_done, n * NQ + last_quad[k] + 1)
                        if k == 1:
                            act.wait_ge(o_turned, 2 * n + 1)
                        nc.scalar.copy(ot[:], ps[:, O_BANK, :]).then_inc(evicted, 1)

            act.wait_ge(fills, FILLS)
            with act.Fori(0, N // 2 - 1) as pair:
                for par in range(2):
                    step(pair * 2 + par, par, steady)
            step(N - 2, 0, steady)
            step(N - 1, 1, final)

        @block.tensor
        def _(pe):
            def score(u, par):
                h, qt = u // TB, u % TB
                i0 = qt * P
                S = score_banks(u)
                q = qop[0:RS, par, h, i0:i0 + P]

                def mm(a, b, lhs, rhs, start):
                    return nc.tensor.matmul(S[:, a:b], lhs, rhs, start=start, stop=True, skip_group_check=True)

                if i == 0:
                    for a, b in cut(0, i0 + P):
                        mm(a, b, q, kop[0:RS, par, h, a:b], True)
                    return mm(i0, i0 + P, identb[:], tri[:, 0, :], False)
                begun = set()
                for what, a, b, off in score_steps(qt):
                    start = a // CH not in begun
                    begun.add(a // CH)
                    if what == "band":
                        last = mm(a, b, identb[:], band[:, off:off + b - a], start)
                    elif what == "turn":
                        last = mm(a, b, turn[0:RS, par, h, i0:i0 + P], kop[0:RS, par, 0, a:b], start)
                    else:
                        last = mm(a, b, q, kop[0:RS, par, 0 if what == "left" else 1, a:b], start)
                return last

            def shifted(k, par):
                half, kt = quads[k // HG]
                h = k % HG
                lo, hi = columns_of(L, half, kt)
                j0, rows = key_tile(L, kt)
                q = qop[0:RA, par, h, :]

                def mm(a, b, lhs, rhs, start):
                    return nc.tensor.matmul(ps[0:rows, T_BANK + k % 2, a % CH:a % CH + b - a], lhs, rhs, start=start,
                                            stop=True, skip_group_check=True)

                if i == 0:
                    last = mm(lo, hi, kop[0:RA, par, h, j0:j0 + P], q[:, lo:hi], True)
                    return mm(j0, j0 + P, identb[:], tri[:, 1, :], False) if lo == j0 else last
                start = True
                for v, a, b in ((1, 0, j0 + WIN), (2, j0 + WIN, j0 + 3 * WIN), (0, j0 + 3 * WIN, T)):
                    a, b = max(a, lo), min(b, hi)
                    if a < b:
                        last = mm(a, b, kop[0:RA, par, v, j0:j0 + rows], q[:, a:b], start)
                        start = False
                a, b = max(j0 - WIN, lo), min(j0 + P + WIN, hi)
                if a < b:
                    off = a - (j0 - WIN)
                    last = mm(a, b, identb[:, 0:rows], band[:, off:off + b - a], False)
                return last

            def values(qd, par):
                half, kt = quads[qd]
                lo, hi = columns_of(L, half, kt)
                vt_ = kt if key_tile(L, kt)[1] == P else TB
                opening = qd == 0 or quads[qd - 1][0] != half
                uniform = opening and i == 1 and half == 0
                if uniform:
                    for t in range(TB):
                        for h in range(HG):
                            nc.tensor.matmul(ps[32 * h:32 * h + 32, O_BANK, 0:GLOB], vst[:, par, t, 0, :],
                                             K.ones[:, 0:GLOB], start=(t == 0), stop=True, skip_group_check=True)
                for h in range(HG):
                    last = nc.tensor.matmul(ps[32 * h:32 * h + 32, O_BANK, lo % CH:lo % CH + hi - lo],
                                            vst[:, par, vt_, h % v_heads, :],
                                            prob[:, qd % 2, h, lo % CH:lo % CH + hi - lo],
                                            start=opening and not uniform, stop=True, skip_group_check=True)
                return last

            def step(n, par, steps, rounds):
                for what, k in steps:
                    if what == "max":
                        if k == 0:
                            pe.wait_ge(loaded[1 - par], rounds * (16 * group_loads))
                        if steps is not first or k >= 2:
                            pe.wait_ge(max_done, (n + 1) * NU + k - 1)
                        score(k, 1 - par).then_inc(s_full, 1)
                    elif what == "rows":
                        pe.wait_ge(m_cut, n + 2)
                        if steps is not first:
                            pe.wait_ge(normed, 2 * n + 1)
                        nc.tensor.transpose(ps[:, SIDE, :].bitcast(BF16)[:, 0:P],
                                            mpart[:].rearrange("p k u -> p (k u)"), identb[:]).then_inc(m_turned, 1)
                    elif what == "exp":
                        if k == 0:
                            pe.wait_ge(m_sent, 32 * (n + 1))
                            pe.wait_ge(v_staged, (n + 1) * (1 + i))
                        if k >= 2:
                            pe.wait_ge(exp_done, n * NX + k - 1)
                        shifted(k, par).then_inc(t_full, 1)
                    elif what == "values":
                        half = quads[k][0]
                        if k > 0 and quads[k - 1][0] != half:
                            pe.wait_ge(evicted, 2 * n + 1)
                        pe.wait_ge(exp_done, n * NX + HG * (k + 1))
                        values(k, par).then_inc(values_done, 1)
                    elif what == "norm":
                        pe.wait_ge(evicted, 2 * n + k + 1)
                        if k == 1 or steps is final:
                            pe.wait_ge(normed, 2 * n + k)
                        if k == 0 or steps is not final:
                            pe.wait_ge(m_copied, n + 1 + k)
                        for j in range(CT):
                            last = nc.tensor.transpose(ps[:, SIDE, j * P:(j + 1) * P], ot[:, j * P:(j + 1) * P],
                                                       ident[:])
                        last.then_inc(o_turned, 1)

            pe.wait_ge(fills, FILLS)
            pe.wait_ge(const_rows, 16 * 2 * L.key_sets * (1 + i))
            step(-1, 1, first, 1)
            with pe.Fori(0, N // 2 - 1) as pair:
                for par in range(2):
                    step(pair * 2 + par, par, steady, pair + 1 + par)
            step(N - 2, 0, steady, N // 2)
            step(N - 1, 1, final, N // 2)


def feed_forward(nc, sem, sb, K, L, dram):
    i = L.index
    tag = str(i)
    ps, x, attn, ident = K.ps, K.x, K.attn, K.ident
    last_layer = i == 1
    wo_loaded = sem("wo_loaded" + tag)
    a_full = sem("a_full" + tag)
    a_done = sem("a_done" + tag)
    y_full = sem("y_full" + tag)
    y_read = sem("y_read" + tag)
    stat = sem("stat" + tag)
    mean_done = sem("mean_done" + tag)
    rstd = sem("rstd" + tag)
    eps_done = sem("eps_done" + tag)
    normal = sem("normal" + tag)
    n_full = sem("n_full" + tag)
    n_hi = sem("n_hi" + tag)
    n_lo = sem("n_lo" + tag)
    up_full = sem("up_full" + tag)
    gate_full = sem("gate_full" + tag)
    silu_done = sem("silu_done" + tag)
    hid = sem("hid" + tag)
    h_hi = sem("h_hi" + tag)
    h_lo = sem("h_lo" + tag)
    down_full = sem("down_full" + tag)
    stored = sem("stored" + tag)
    pairs = [(0, 0), (0, 1)] if i == 0 else [(0, 0), (0, 1), (1, 0)]
    with ExitStack() as st:
        wo = sb(st, "wo" + tag, [P, KD, D], F32)
        at = sb(st, "at" + tag, [P, KD, CH], F32)
        xs = sb(st, "xs" + tag, [P, 2, KD, TOK], F32R)
        hs = sb(st, "hs" + tag, [P, KE, 2, CH], F32R)
        sg = sb(st, "sg" + tag, [P, 2, CH], F32)
        hf = sb(st, "hf" + tag, [P, 2, CH], F32)
        stats = sb(st, "stats" + tag, [P, NT, 6], F32)
        mv = sb(st, "mv" + tag, [P, 2, NT, 2], F32)
        inv = sb(st, "inv" + tag, [P, 2, 2, NT], F32)
        w = K.wffn
        wup = [w[:, 0, s, :].rearrange("p (k n) -> p k n", k=KD) for s in range(1 + i)]
        wgate = [w[:, 1, s, :].rearrange("p (k n) -> p k n", k=KD) for s in range(1 + i)]
        wdown = [w[:, 2, s, :].rearrange("p (k n) -> p k n", k=KE) for s in range(1 + i)]
        out_dst = dram.out.rearrange("(t p) d -> p t d", p=P)
        block = st.enter_context(nc.Block())

        @block.sync
        def _(sp):
            sp.dma_start(wo[:], dram.wo[i].rearrange("(k p) n -> p k n", p=P)).then_inc(wo_loaded, 16)
            if last_layer:
                for c in range(NC):
                    sp.wait_ge(normal, NT + CT * (c + 1))
                    sp.dma_start(out_dst[:, CT * c:CT * c + CT, :], x[:, CT * c:CT * c + CT, :]).then_inc(stored, 16)
                sp.wait_ge(stored, 16 * NC)

        @block.gpsimd
        def _(pool):
            def inverse(c, second):
                tiles = slice(CT * c, CT * c + CT)
                m = c + NC * second
                pool.wait_ge(mean_done, CT * (m + 1))
                nc.gpsimd.tensor_scalar(inv[:, second, 0, tiles], mv[:, second, tiles, 1], LN_EPS, 0.0, ALU.add,
                                        ALU.add).then_inc(eps_done, 1)
                pool.wait_ge(eps_done, m + 1)
                nc.gpsimd.tensor_tensor(inv[:, second, 1, tiles], inv[:, second, 0, tiles], K.power[:],
                                        ALU.pow).then_inc(rstd, 1)

            for c in range(NC):
                inverse(c, 0)
            for c in range(NC):
                for e in range(KE):
                    u = c * KE + e
                    pool.wait_ge(h_hi, u + 1)
                    nc.gpsimd.tensor_tensor(hs[:, e, 1, :], hf[:, u % 2, :], hs[:, e, 0, :].bitcast(F32),
                                            ALU.subtract).then_inc(h_lo, 1)
                    if e == 3 and c >= 1:
                        inverse(c - 1, 1)
            inverse(NC - 1, 1)

        @block.scalar
        def _(act):
            def high(c):
                for k in range(KD):
                    n = c * KD + k
                    act.wait_ge(n_full, n + 1)
                    nc.scalar.copy(xs[:, 0, k, c * CH:(c + 1) * CH], ps[:, 4 + n % 2, :]).then_inc(n_hi, 1)

            for c in range(NC):
                for k in range(KD):
                    n = c * KD + k
                    act.wait_ge(a_full, n + 1)
                    if c >= 1:
                        act.wait_ge(y_full, 2 * c)
                    nc.scalar.copy(at[:, k, :], ps[:, n % 2, :]).then_inc(a_done, 1)
                if c >= 1:
                    high(c - 1)
            high(NC - 1)

            def round_hidden(u):
                c, e = u // KE, u % KE
                act.wait_ge(hid, u + 1)
                if c >= 1 and e == 0:
                    act.wait_ge(down_full, 2 * c)
                nc.scalar.copy(hs[:, e, 0, :], hf[:, u % 2, :]).then_inc(h_hi, 1)

            for u in range(NC * KE):
                act.wait_ge(up_full, u + 1)
                if u >= 2:
                    act.wait_ge(hid, u - 1)
                nc.scalar.activation(sg[:, u % 2, :], ps[:, 2 * (u % 2), :], ACT.Silu,
                                     scale=K.scales[:, 0:1] if i == 0 else 1.0).then_inc(silu_done, 1)
                if u >= 1:
                    round_hidden(u - 1)
            round_hidden(NC * KE - 1)

        @block.vector
        def _(dve):
            def add_and_measure(c, second):
                for hf_ in range(2):
                    t0 = CT * c + 2 * hf_
                    dst = x[:, t0:t0 + 2, :].rearrange("p t d -> p (t d)")
                    if not second:
                        dve.wait_ge(y_full, 2 * c + hf_ + 1)
                        nc.vector.tensor_tensor(dst, ps[:, 2 + hf_, :], dst, ALU.add).then_inc(y_read, 1)
                    else:
                        dve.wait_ge(down_full, 2 * c + hf_ + 1)
                        nc.vector.scalar_tensor_tensor(out=dst, in0=ps[:, 4 + hf_, :],
                                                       scalar=K.scales[:, 2:3] if i == 0 else 1.0, in1=dst,
                                                       op0=ALU.mult, op1=ALU.add).then_inc(y_read, 1)
                m = (c + NC * second)
                for t in range(CT):
                    dve.wait_ge(y_read, 2 * m + t // 2 + 1)
                    nc.vector.bn_stats(stats[:, CT * c + t, :], x[:, CT * c + t, :]).then_inc(stat, 1)
                for t in range(CT):
                    dve.wait_ge(stat, CT * m + t + 1)
                    nc.vector.bn_aggr(mv[:, second, CT * c + t, :], stats[:, CT * c + t, :]).then_inc(mean_done, 1)

            def normalise(c, second):
                m = c + NC * second
                dve.wait_ge(rstd, m + 1)
                dve.wait_ge(mean_done, CT * (m + 1))
                for t in range(CT * c, CT * c + CT):
                    nc.vector.tensor_scalar(x[:, t, :], x[:, t, :], mv[:, second, t, 0:1],
                                            inv[:, second, 1, t:t + 1], ALU.subtract, ALU.mult).then_inc(normal, 1)

            def low(c):
                for k in range(KD):
                    n = c * KD + k
                    dve.wait_ge(n_hi, n + 1)
                    nc.vector.tensor_tensor(xs[:, 1, k, c * CH:(c + 1) * CH], ps[:, 4 + n % 2, :],
                                            xs[:, 0, k, c * CH:(c + 1) * CH].bitcast(F32), ALU.subtract).then_inc(n_lo, 1)

            for c in range(NC):
                add_and_measure(c, 0)
                if c >= 1:
                    normalise(c - 1, 0)
                if c >= 2:
                    low(c - 2)
            normalise(NC - 1, 0)
            low(NC - 2)
            low(NC - 1)
            for c in range(NC):
                for e in range(KE):
                    u = c * KE + e
                    dve.wait_ge(gate_full, u + 1)
                    dve.wait_ge(silu_done, u + 1)
                    if u >= 2:
                        dve.wait_ge(h_lo, u - 1)
                    nc.vector.scalar_tensor_tensor(out=hf[:, u % 2, :], in0=ps[:, 2 * (u % 2) + 1, :],
                                                   scalar=K.scales[:, 1:2] if i == 0 else 1.0, in1=sg[:, u % 2, :],
                                                   op0=ALU.mult, op1=ALU.mult).then_inc(hid, 1)
                    if c >= 1 and e == 1:
                        add_and_measure(c - 1, 1)
                    if c >= 1 and e == 5:
                        normalise(c - 1, 1)
            add_and_measure(NC - 1, 1)
            normalise(NC - 1, 1)

        @block.tensor
        def _(pe):
            def project_chunk(c):
                for k in range(KD):
                    n = c * KD + k
                    if n >= 2:
                        pe.wait_ge(a_done, n - 1)
                    for j in range(CT):
                        t = CT * c + j
                        last = nc.tensor.transpose(ps[:, n % 2, j * P:(j + 1) * P], attn[:, (t // TB) * KD + k, t % TB, :],
                                                   ident[:])
                    last.then_inc(a_full, 1)
                pe.wait_ge(a_done, KD * (c + 1))
                for half in range(2):
                    if c >= 1:
                        pe.wait_ge(y_read, 2 * (c - 1) + half + 1)
                    for j in range(2 * half, 2 * half + 2):
                        for k in range(KD):
                            last = nc.tensor.matmul(ps[:, 2 + half, (j % 2) * D:(j % 2 + 1) * D],
                                                    at[:, k, j * P:(j + 1) * P], wo[:, k, :],
                                                    start=(k == 0), stop=(k == KD - 1))
                    last.then_inc(y_full, 1)

            def turn_chunk(c):
                pe.wait_ge(normal, CT * (c + 1))
                for k in range(KD):
                    n = c * KD + k
                    if n >= 2:
                        pe.wait_ge(n_lo, n - 1)
                    for j in range(CT):
                        last = nc.tensor.transpose(ps[:, 4 + n % 2, j * P:(j + 1) * P],
                                                   x[:, CT * c + j, k * P:(k + 1) * P], ident[:])
                    last.then_inc(n_full, 1)

            def unit(u):
                c, e = u // KE, u % KE
                for which, weights, full in ((0, wup, up_full), (1, wgate, gate_full)):
                    if u >= 2:
                        pe.wait_ge(silu_done if which == 0 else hid, u - 1)
                    n = 0
                    for k in range(KD):
                        for a, b in pairs:
                            last = nc.tensor.matmul(ps[:, 2 * (u % 2) + which, :],
                                                    weights[a][:, k, e * P:(e + 1) * P],
                                                    xs[:, b, k, c * CH:(c + 1) * CH],
                                                    start=(n == 0), stop=(n == KD * len(pairs) - 1))
                            n += 1
                    last.then_inc(full, 1)

            def down(c):
                pe.wait_ge(h_lo, KE * (c + 1))
                for half in range(2):
                    if c >= 1:
                        pe.wait_ge(y_read, 2 * NC + 2 * (c - 1) + half + 1)
                    for j in range(2 * half, 2 * half + 2):
                        n = 0
                        for e in range(KE):
                            for a, b in pairs:
                                last = nc.tensor.matmul(ps[:, 4 + half, (j % 2) * D:(j % 2 + 1) * D],
                                                        hs[:, e, b, j * P:(j + 1) * P], wdown[a][:, e, :],
                                                        start=(n == 0), stop=(n == KE * len(pairs) - 1))
                                n += 1
                    last.then_inc(down_full, 1)

            pe.wait_ge(wo_loaded, 16)
            for c in range(NC):
                project_chunk(c)
                if c >= 1:
                    turn_chunk(c - 1)
            turn_chunk(NC - 1)
            pe.wait_ge(n_lo, KD * NC)
            pe.wait_ge(y_read, 2 * NC)
            unit(0)
            unit(1)
            for c in range(NC):
                for u in range(c * KE + 2, min((c + 1) * KE + 2, NC * KE)):
                    unit(u)
                down(c)


def one(n):
    return slice(n, n + 1) if isinstance(n, int) else bass.ds(n, 1)


def build(nc, dram):
    layers = (Layer(0), Layer(1))
    dram.q_parts = [nc.dram_tensor(f"q_parts{i}", (PARTS, B, D, T), BF16, kind="Internal").ap() for i in range(2)]
    dram.k_parts = [nc.dram_tensor(f"k_parts{i}", (PARTS, B, layers[i].kv_width, T), BF16, kind="Internal").ap()
                    for i in range(2)]
    with ExitStack() as top:
        def sb(stack, name, shape, dt):
            return stack.enter_context(nc.sbuf_tensor(name, shape, dt))

        def sem(name):
            return top.enter_context(nc.semaphore(name))

        K = Chip()
        K.ps = top.enter_context(nc.psum_tensor("ps", [P, 8, CH], F32))
        K.x = sb(top, "x", [P, NT, D], F32)
        K.ident = sb(top, "ident", [P, P], F32)
        K.identb = sb(top, "identb", [P, P], BF16)
        K.tri = sb(top, "tri", [P, 2, P], BF16)
        K.band = sb(top, "band", [P, P + 2 * WIN], BF16)
        K.ones = sb(top, "ones", [P, P], F32)
        K.power = sb(top, "power", [P, CT], F32)
        K.scales = sb(top, "scales", [P, 3], F32)
        K.bias = sb(top, "bias", [P, 2, D], F32)
        for L in layers:
            with ExitStack() as layer:
                K.wffn = sb(layer, f"ffn_parts{L.index}", [P, 3, 1 + L.index, KD * E], F32R)
                K.attn = sb(layer, f"attn{L.index}", [P, N // 2, TB, P], F32)
                with ExitStack() as values:
                    K.v_all = sb(values, f"v_all{L.index}", [P, N, TB, L.kv_width // NG], F32)
                    project(nc, sem, sb, K, L, dram)
                    attend(nc, sem, sb, K, L, dram)
                feed_forward(nc, sem, sb, K, L, dram)


def bf16_bits(a):
    u = np.ascontiguousarray(a, np.float32).view(np.uint32)
    return ((u + 0x7FFF + ((u >> 16) & 1)) >> 16).astype(np.uint16)


def three_parts(a):
    parts = []
    for _ in range(PARTS):
        p = (bf16_bits(a).astype(np.uint32) << 16).view(np.float32)
        parts.append(p)
        a = a - p
    return parts


def constants():
    r = np.arange(P)
    tri = np.where(r[None, :] > r[:, None], -1e30, 0.0)
    c = np.arange(P + 2 * WIN)
    band = np.where(np.abs(c[None, :] - WIN - r[:, None]) <= WIN, -1e9, 0.0)
    pos = np.arange(T)
    high, low, unit = (pos // P * P).astype(np.float32), (pos % P).astype(np.float32), np.ones(T, np.float32)
    left = np.stack([high] * 3 + [low] * 3 + [unit] * 3)
    mixed = np.where(((pos - GLOB) // GLOB) % 2 == 0, 1.0, -1.0).astype(np.float32)
    kpos = np.stack([left, -left, left * mixed], axis=1)
    slopes = np.float32(2.0 ** (-(2.0 ** -(np.log2(H) - 3.0)))) ** np.arange(1, H + 1, dtype=np.float32)
    s = three_parts(slopes)
    g = three_parts(-(slopes[:, None] * pos[None, :].astype(np.float32)))
    qpos = np.stack([np.broadcast_to(a[:, None], (H, T)) for a in (*s, *s)] + g).astype(np.float32)
    late = (pos % P >= P // 2).astype(np.float32)

    def by_group(a):
        a = a.reshape(NPOS, NG, HG, T).transpose(1, 0, 2, 3)
        return np.concatenate([a] * B)

    return {
        "ident": np.eye(P, dtype=np.float32), "identb": bf16_bits(np.eye(P)),
        "tri": bf16_bits(np.stack([tri, tri.T], axis=1)), "band": bf16_bits(band), "kpos": bf16_bits(kpos),
        "qpos": bf16_bits(by_group(qpos)), "qturn": bf16_bits(by_group(2.0 * qpos * late)),
    }


def kernel(**inputs):
    import concourse.bacc as bacc
    from concourse.bass_utils import run_bass_kernel_spmd as run

    a = {k: np.asarray(v) for k, v in inputs.items()}
    arrays = {
        "x": a["L0_attn_x"].reshape(TOK, D),
        "w_qkv0": a["L0_attn_w_qkv"], "w_out0": a["L0_attn_w_out"], "b_out0": a["L0_attn_b_out"].reshape(1, D),
        "up0": a["L0_ffn_W_up"].T, "gate0": a["L0_ffn_W_gate"].T, "down0": a["L0_ffn_W_down"].T,
        "w_q1": a["L1_attn_Wq"], "w_kv1": a["L1_attn_Wkv"], "w_out1": a["L1_attn_Wo"],
        "b_out1": a["L1_attn_bo"].reshape(1, D),
        "gate1": a["L1_ffn_w_gate"].T, "up1": a["L1_ffn_w_up"].T, "down1": a["L1_ffn_w_down"].T,
        **constants(),
    }
    arrays = {k: np.ascontiguousarray(v) for k, v in arrays.items()}
    nc = bacc.Bacc("TRN2", target_bir_lowering=False, num_devices=1)
    t = {k: nc.dram_tensor("in_" + k, v.shape, mybir.dt.from_np(v.dtype), kind="ExternalInput").ap()
         for k, v in arrays.items()}
    t = {k: v.bitcast(BF16) if v.dtype == mybir.dt.uint16 else v for k, v in t.items()}
    out = nc.dram_tensor("out", (TOK, D), F32, kind="ExternalOutput").ap()
    dram = Dram()
    dram.x, dram.out = t["x"], out
    dram.ident, dram.identb, dram.tri, dram.band = t["ident"], t["identb"], t["tri"], t["band"]
    dram.kpos, dram.qpos, dram.qturn = t["kpos"], t["qpos"], t["qturn"]
    dram.wq, dram.wkv = (t["w_qkv0"], t["w_q1"]), t["w_kv1"]
    dram.wo, dram.bias = (t["w_out0"], t["w_out1"]), (t["b_out0"], t["b_out1"])
    dram.ffn = ((t["up0"], t["gate0"], t["down0"]), (t["gate1"], t["up1"], t["down1"]))
    build(nc, dram)
    r = run(nc, [{"in_" + k: v for k, v in arrays.items()}], core_ids=[0])
    return r.results[0]["out"].reshape(B, T, D)
```

```python
from contextlib import ExitStack

import numpy as np
import concourse.bass as bass
from concourse import mybir

ALU = mybir.AluOpType
ACT = mybir.ActivationFunctionType
AX = mybir.AxisListType
F32 = mybir.dt.float32
F32R = mybir.dt.float32r
BF16 = mybir.dt.bfloat16

P = 128
B, T, D = 2, 1024, 256
TOK = B * T
NT = TOK // P
TB = T // P
KD = D // P
H, HD = 16, 16
HG = 4
NG = H // HG
N = B * NG
E = 1024
KE = E // P
CH = 512
NC = TOK // CH
RING = 4
CT = CH // P
WIN, GLOB = 32, 64
PARTS = 3
Q_PART = (0, 0, 0, 1, 1, 2)
K_PART = (0, 1, 2, 0, 1, 0)
NPAIR = len(Q_PART)
BUFS = 3
NPOS = 9
LN_EPS = 1e-5
QUANT_EPS = 1e-8


class Chip:
    pass


class Dram:
    pass


class Layer:

    def __init__(self, index):
        self.index = index
        self.first_row = 0 if index == 0 else NPOS
        self.score_rows = self.first_row + NPAIR * HD
        self.rows = self.score_rows + 2
        self.key_sets = HG if index == 0 else 3
        self.kv_width = D if index == 0 else D // HG


def maximum_columns(layer, qt):
    return (0, (qt + 1) * P) if layer.index == 0 else (GLOB, T)


def cut(lo, hi):
    return [(a, min(b, hi)) for a, b in ((max(lo, c), c + CH) for c in range(0, T, CH)) if a < min(b, hi)]


def score_steps(qt):
    i0 = qt * P
    turn = max(GLOB, i0 + WIN)
    steps = [("left", a, b, 0) for a, b in cut(GLOB, turn)]
    steps += [("right", a, b, 0) for a, b in cut(turn, T)]
    steps += [("turn", a, b, 0) for a, b in cut(turn, i0 + 3 * WIN)]
    steps += [("band", a, b, a - (i0 - WIN)) for a, b in cut(max(GLOB, i0 - WIN), min(T, i0 + P + WIN))]
    return sorted(steps, key=lambda s: s[1] // CH)


def key_tile(layer, kt):
    if layer.index == 0:
        return kt * P, P
    j0 = GLOB + kt * P
    return j0, min(P, T - j0)


def columns_of(layer, half, kt):
    lo, hi = half * CH, (half + 1) * CH
    return (max(lo, kt * P), hi) if layer.index == 0 else (max(lo, GLOB), hi)


def quads_of(layer):
    return [(half, kt) for half in range(2) for kt in range(TB)
            if columns_of(layer, half, kt)[0] < columns_of(layer, half, kt)[1]]


def plan(layer, late, scores, values, ends):
    units = list(range(HG * TB)) if scores else []
    if not values:
        return [("max", u, 1) for u in units] + [("rows", 0, 1)]
    quads = quads_of(layer)
    nq = len(quads)
    steps, given = [], 0
    tail = [("values", nq - 1), ("evict", 1), ("norm", 1)]
    rows_at = nq - 3
    for n, (half, kt) in enumerate(quads):
        due = min(len(units), -(-len(units) * (n + 1) // rows_at))
        for h in range(HG):
            steps.append(("exp", HG * n + h, 0))
            upto = given + -(-(due - given) // (HG - h))
            steps += [("max", u, 1) for u in units[given:upto]]
            given = upto
        if n == 0 and late:
            steps += [(what, k, -1) for what, k in tail[:2]]
        if n == 1 and late:
            steps.append((*tail[2], -1))
        if n >= 1:
            steps.append(("values", n - 1, 0))
            if quads[n - 1][0] != half:
                steps.append(("evict", quads[n - 1][0], 0))
        if n >= 2 and quads[n - 2][0] != quads[n - 1][0]:
            steps.append(("norm", quads[n - 2][0], 0))
        if units and n == rows_at:
            steps.append(("rows", 0, 1))
    if ends:
        steps += [(what, k, 0) for what, k in tail]
    return steps


def project(nc, sem, sb, K, L, dram):
    i = L.index
    tag = str(i)
    ps, x, ident = K.ps, K.x, K.ident
    x_loaded = [sem(f"x_loaded{c}") for c in range(NC)] if i == 0 else None
    ident_loaded = sem("ident_loaded") if i == 0 else None
    const_loaded = sem("const_loaded") if i == 0 else None
    w_loaded = sem("wqkv_loaded" + tag)
    ffn_loaded = [sem(f"ffn_loaded{tag}{j}") for j in range(3)] if i == 0 else None
    xt_full = sem("xt_full" + tag)
    xt_act = sem("xt_act" + tag)
    xt_dve = sem("xt_dve" + tag)
    proj_full = sem("proj_full" + tag)
    part1 = sem("part1_done" + tag)
    rest1 = sem("rest1_done" + tag)
    part2 = sem("part2_done" + tag)
    part3 = sem("part3_done" + tag)
    sent = [sem(f"parts_sent{tag}{k}") for k in range(RING)]
    v_full = sem("v_full" + tag)
    v_done = sem("v_done" + tag)
    vt_done = sem("vt_done" + tag)
    cw_step = sem("cw_step" + tag)
    xc_ready = sem("xc_ready" + tag)
    ones_set = sem("ones_set" + tag)
    abs_sum = sem("abs_sum" + tag)
    total = sem("abs_total" + tag)
    tern = sem("ternary_step" + tag)

    NW = 3 * D if i == 0 else D + 2 * L.kv_width
    with ExitStack() as st:
        xt = sb(st, "xt" + tag, [P, KD, TOK], F32)
        w = sb(st, "wqkv" + tag, [P, KD, NW], F32)
        part = sb(st, "part" + tag, [P, RING, PARTS, CH], BF16)
        rest = sb(st, "rest" + tag, [P, RING, CH], F32)
        if i == 0:
            wf = sb(st, "wffn", [P, 3, KD * E], F32)
            wsum = sb(st, "wsum", [P, 3], F32)
            thr = sb(st, "thr", [P, 2, 3], F32)
            below = sb(st, "below", [P, KD * E], F32)
            units = [(b, m, c) for b in range(B) for m in range(2 * KD) for c in range(2)]
            v_units = [(b, c) for b in range(B) for c in range(TB // 2)]
        else:
            xct = sb(st, "xct", [P, KD, TOK], F32)
            xc = sb(st, "xc", [P, CT, D], F32)
            vt = sb(st, "vt", [P, B, T + GLOB], F32)
            cw = sb(st, "cw", [P, 4, NT], F32)
            units = [(b, m, c) for b in range(B) for m in (KD, 0, 1) for c in range(2)]
            v_units = list(range(B))
        turns = [(c, s, k) for c in range(NC) for s in range(1 + i) for k in range(KD)]

        def is_q(m):
            return m < KD

        def rows_of(m):
            return P if i == 0 or is_q(m) else L.kv_width

        def sent_before(u, k):
            return sum(1 if i == 0 or is_q(m) else L.key_sets
                       for w_, (_, m, _) in enumerate(units[:u]) if w_ % RING == k)

        if i == 0:
            order = [o for u in range(0, len(units), 2) for o in (("qk", u), ("qk", u + 1), ("v", u // 2))]
        else:
            order = [("qk", u) for u in range(len(units))]
            order[4:4] = [("v", 0)]
            order += [("v", 1)]
        block = st.enter_context(nc.Block())

        @block.sync
        def _(sp):
            if i == 0:
                xv = dram.x.rearrange("(t p) d -> p t d", p=P)
                sp.dma_start(ident[:], dram.ident).then_inc(ident_loaded, 16)
                for c in range(NC):
                    sp.dma_start(x[:, CT * c:CT * c + CT, :], xv[:, CT * c:CT * c + CT, :]).then_inc(x_loaded[c], 16)
            for u, (b, m, c) in enumerate(units):
                sp.wait_ge(part3, u + 1)
                sp.wait_ge(part2, u + 1)
                r = rows_of(m)
                cols = slice(c * CH, (c + 1) * CH)
                if i == 0 or is_q(m):
                    g0 = b * NG + (m % KD) * (NG // KD)
                    dst = (dram.q_parts if is_q(m) else dram.k_parts)[i][:, g0:g0 + NG // KD]
                    dst = dst.rearrange("k g d (h t) -> (g d h) k t", t=T)[:, :, cols]
                    sp.dma_start(dst, part[0:r, u % RING, :, :]).then_inc(sent[u % RING], 16)
                else:
                    dst = dram.k_parts[i][:, b * NG:(b + 1) * NG].rearrange("k g d (s t) -> s (g d) k t", t=T)
                    for s in range(L.key_sets):
                        sp.dma_start(dst[s, :, :, cols], part[0:r, u % RING, :, :]).then_inc(sent[u % RING], 16)
            for k in range(RING):
                sp.wait_ge(sent[k], 16 * sent_before(len(units), k))

        if i == 0:
            @block.gpsimd
            def _(pool):
                nc.gpsimd.memset(K.ones[:], 1.0).then_inc(ones_set, 1)
                nc.gpsimd.memset(K.power[:], -0.5).then_inc(ones_set, 1)
                pool.wait_ge(x_loaded[NC - 1], 16)
                for j, wt in enumerate(dram.ffn[0]):
                    wt = wt.rearrange("(k p) n -> p k n", p=P)
                    pool.dma_start(wf[:, j, :].rearrange("p (k n) -> p k n", k=wt.shape[1]), wt
                                   ).then_inc(ffn_loaded[j], 16)
                pool.dma_start(K.identb[:], dram.identb).then_inc(const_loaded, 16)
                pool.dma_start(K.tri[:], dram.tri).then_inc(const_loaded, 16)
                pool.dma_start(K.band[:], dram.band).then_inc(const_loaded, 16)
                for j in range(2):
                    pool.dma_start(K.bias[:, j, :], dram.bias[j].to_broadcast((P, D))).then_inc(const_loaded, 16)
                pool.wait_ge(const_loaded, 16 * 5)

        @block.scalar
        def _(act):
            if i == 0:
                act.dma_start(w[:], dram.wq[0].rearrange("(k p) n -> p k n", p=P)).then_inc(w_loaded, 16)
            else:
                act.dma_start(w[:, :, 0:D], dram.wq[1].rearrange("(k p) n -> p k n", p=P)).then_inc(w_loaded, 16)
                act.dma_start(w[:, :, D:NW], dram.wkv.rearrange("(k p) n -> p k n", p=P)).then_inc(w_loaded, 16)
                act.wait_ge(cw_step, 1)
                nc.scalar.activation(cw[:, 1, :], cw[:, 0, :], ACT.Exp, scale=-1.0).then_inc(cw_step, 1)
            for n, (c, s, k) in enumerate(turns):
                if k == 0:
                    act.wait_ge(xt_full, n + 1)
                    dst = xct if s else xt
                    nc.scalar.copy(dst[:, k, c * CH:(c + 1) * CH], ps[:, n % 2, :]).then_inc(xt_act, 1)

            def second_part(u):
                r = rows_of(units[u][1])
                act.wait_ge(rest1, u + 1)
                nc.scalar.copy(part[0:r, u % RING, 1, :], rest[0:r, u % RING, :]).then_inc(part2, 1)

            for what, u in order:
                if what == "v":
                    act.wait_ge(v_full, u + 1)
                    if i == 0:
                        b, c = v_units[u]
                        for j in range(2):
                            nc.scalar.copy(K.v_all[:, b * NG:(b + 1) * NG, 2 * c + j, :],
                                           ps[:, 6 + u % 2, j * D:(j + 1) * D].rearrange("p (g d) -> p g d", g=NG)
                                           ).then_inc(v_done, 1)
                    else:
                        nc.scalar.copy(K.v_all[:, u * NG:(u + 1) * NG, :, :],
                                       ps[:, 6 + u, :].rearrange("p (t g d) -> p g t d", t=TB, g=NG)
                                       ).then_inc(v_done, 1)
                    continue
                b, m, c = units[u]
                r = rows_of(m)
                act.wait_ge(proj_full, u + 1)
                if u >= RING:
                    act.wait_ge(sent[u % RING], 16 * sent_before(u, u % RING))
                nc.scalar.activation(part[0:r, u % RING, 0, :], ps[0:r, 2 + u % 4, :], ACT.Copy,
                                     scale=0.25 if is_q(m) else 1.0).then_inc(part1, 1)
                if i == 1 and not is_q(m):
                    nc.scalar.copy(vt[r:P, b, c * CH:(c + 1) * CH], ps[r:P, 2 + u % 4, :]).then_inc(vt_done, 1)
                    if c == 0:
                        nc.scalar.copy(vt[r:P, b, T:T + GLOB], ps[r:P, 2 + u % 4, 0:GLOB]).then_inc(vt_done, 1)
                if u >= 1:
                    second_part(u - 1)
            second_part(len(units) - 1)

        @block.vector
        def _(dve):
            if i == 1:
                nc.vector.tensor_reduce(cw[:, 0, :], x[:], AX.X, ALU.add,
                                        apply_absolute_value=True).then_inc(cw_step, 1)
                dve.wait_ge(cw_step, 2)
                nc.vector.tensor_scalar(cw[:, 2, :], cw[:, 1, :], 1.0, None, ALU.add).then_inc(cw_step, 1)
                dve.wait_ge(cw_step, 3)
                nc.vector.reciprocal(cw[:, 3, :], cw[:, 2, :]).then_inc(cw_step, 1)
                dve.wait_ge(cw_step, 4)

            def scaled(c):
                if c >= 1:
                    dve.wait_ge(xt_full, turns.index((c - 1, 1, 1)) + 1)
                for t in range(CT):
                    nc.vector.tensor_scalar(xc[:, t, :], x[:, CT * c + t, :], cw[:, 3, CT * c + t:CT * c + t + 1],
                                            None, ALU.mult).then_inc(xc_ready, 1)

            for n, (c, s, k) in enumerate(turns):
                if i == 1 and s == 0 and k == 0:
                    scaled(c)
                if k == 1:
                    dve.wait_ge(xt_full, n + 1)
                    dst = xct if s else xt
                    nc.vector.tensor_copy(dst[:, k, c * CH:(c + 1) * CH], ps[:, n % 2, :]).then_inc(xt_dve, 1)

            def third_part(u):
                r = rows_of(units[u][1])
                dve.wait_ge(part2, u + 1)
                nc.vector.tensor_tensor(part[0:r, u % RING, 2, :], rest[0:r, u % RING, :], part[0:r, u % RING, 1, :],
                                        ALU.subtract).then_inc(part3, 1)

            def ternary(piece):
                if piece < 3:
                    j = piece
                    dve.wait_ge(ffn_loaded[j], 16)
                    nc.vector.tensor_reduce(wsum[:, j:j + 1], wf[:, j, :], AX.X, ALU.add,
                                            apply_absolute_value=True).then_inc(abs_sum, 1)
                elif piece == 3:
                    dve.wait_ge(total, 1)
                    nc.vector.tensor_scalar(K.scales[:], ps[:, 0, 0:3], 1.0 / (D * E), QUANT_EPS, ALU.mult,
                                            ALU.add).then_inc(tern, 1)
                    dve.wait_ge(tern, 1)
                    for s in range(2):
                        nc.vector.tensor_scalar(thr[:, s, :], K.scales[:], 0.5 - s, None, ALU.mult).then_inc(tern, 1)
                else:
                    j = piece - 4
                    dve.wait_ge(tern, 3 + 2 * j)
                    nc.vector.tensor_scalar(below[:], wf[:, j, :], thr[:, 1, j:j + 1], None, ALU.is_lt).then_inc(tern, 1)
                    dve.wait_ge(tern, 4 + 2 * j)
                    nc.vector.scalar_tensor_tensor(out=K.wffn[:, j, 0, :], in0=wf[:, j, :], scalar=thr[:, 0, j:j + 1],
                                                   in1=below[:], op0=ALU.is_gt, op1=ALU.subtract).then_inc(tern, 1)

            for what, u in order:
                if what == "v":
                    if i == 0 and u >= 1:
                        ternary(u - 1)
                    continue
                b, m, c = units[u]
                r = rows_of(m)
                dve.wait_ge(part1, u + 1)
                if u >= RING:
                    dve.wait_ge(part3, u - RING + 1)
                nc.vector.scalar_tensor_tensor(
                    out=rest[0:r, u % RING, :], in0=ps[0:r, 2 + u % 4, :], scalar=0.25 if is_q(m) else 1.0,
                    in1=part[0:r, u % RING, 0, :], op0=ALU.mult, op1=ALU.subtract).then_inc(rest1, 1)
                if u >= 1:
                    third_part(u - 1)
            third_part(len(units) - 1)

        @block.tensor
        def _(pe):
            if i == 0:
                pe.wait_ge(ident_loaded, 16)
            for n, (c, s, k) in enumerate(turns):
                if i == 0 and k == 0:
                    pe.wait_ge(x_loaded[c], 16)
                if s == 1 and k == 0:
                    pe.wait_ge(xc_ready, CT * (c + 1))
                if n >= 2:
                    pe.wait_ge(xt_act if k == 0 else xt_dve, (n - 2) // 2 + 1)
                for j in range(CT):
                    src = xc[:, j, k * P:(k + 1) * P] if s else x[:, CT * c + j, k * P:(k + 1) * P]
                    last = nc.tensor.transpose(ps[:, n % 2, j * P:(j + 1) * P], src, ident[:])
                last.then_inc(xt_full, 1)
            pe.wait_ge(xt_act, len(turns) // 2)
            pe.wait_ge(xt_dve, len(turns) // 2)
            pe.wait_ge(w_loaded, 16 * (1 + i))
            for what, u in order:
                if what == "v":
                    if i == 0:
                        b, c = v_units[u]
                        if u >= 2:
                            pe.wait_ge(v_done, 2 * (u - 1))
                        for j in range(2):
                            t0 = b * T + (2 * c + j) * P
                            for k in range(KD):
                                last = nc.tensor.matmul(ps[:, 6 + u % 2, j * D:(j + 1) * D], xt[:, k, t0:t0 + P],
                                                        w[:, k, 2 * D:3 * D], start=(k == 0), stop=(k == KD - 1))
                        if u == 3:
                            pe.wait_ge(abs_sum, 3)
                            pe.wait_ge(ones_set, 1)
                            nc.tensor.matmul(ps[:, 0, 0:3], K.ones[:], wsum[:], start=True, stop=True
                                             ).then_inc(total, 1)
                    else:
                        pe.wait_ge(vt_done, 3 * (u + 1))
                        for t in range(TB):
                            j0 = GLOB + t * P
                            last = nc.tensor.transpose(ps[:, 6 + u, t * HG * HD:(t + 1) * HG * HD],
                                                       vt[L.kv_width:P, u, j0:j0 + P],
                                                       ident[L.kv_width:P, L.kv_width:P])
                    last.then_inc(v_full, 1)
                    continue
                b, m, c = units[u]
                if u >= 4:
                    pe.wait_ge(rest1, u - 3)
                    copies = sum((2 if cc == 0 else 1) for (_, mm, cc) in units[:u - 3] if mm == KD) if i else 0
                    if copies:
                        pe.wait_ge(vt_done, copies)
                src = xct if i == 1 and is_q(m) else xt
                t0 = b * T + c * CH
                for k in range(KD):
                    last = nc.tensor.matmul(ps[:, 2 + u % 4, :], w[:, k, m * P:(m + 1) * P],
                                            src[:, k, t0:t0 + CH], start=(k == 0), stop=(k == KD - 1))
                last.then_inc(proj_full, 1)


def attend(nc, sem, sb, K, L, dram):
    i = L.index
    tag = str(i)
    ps, attn, ident, identb, tri, band = K.ps, K.attn, K.ident, K.identb, K.tri, K.band
    R0, RS, RA = L.first_row, L.score_rows, L.rows
    quads = quads_of(L)
    NU, NX, NQ = HG * TB, HG * len(quads), len(quads)
    last_quad = [max(q for q in range(NQ) if quads[q][0] == half) for half in range(2)]
    group_loads = 2 * NPAIR + 2 * i
    S_BANK, T_BANK, O_BANK, SIDE = 0, 4, 6, 7
    loaded = [sem(f"operands_loaded{tag}{k}") for k in range(BUFS)]
    fills = sem("constants_filled" + tag)
    FILLS = 2 + 2 * i
    const_rows = sem("constant_rows" + tag)
    v_staged = sem("v_staged" + tag)
    residual = sem("residual" + tag)
    s_full = sem("s_full" + tag)
    max_done = sem("max_done" + tag)
    m_high = sem("m_high" + tag)
    m_cut = sem("m_cut" + tag)
    m_turned = sem("m_turned" + tag)
    m_copied = sem("m_copied" + tag)
    m_sent = sem("m_sent" + tag)
    w_loaded = sem("ffn_loaded1") if i == 1 else None
    w_cut = sem("ffn_weights_cut") if i == 1 else None
    t_full = sem("t_full" + tag)
    exp_done = sem("exp_done" + tag)
    values_done = sem("values_done" + tag)
    evicted = sem("evicted" + tag)
    o_turned = sem("o_turned" + tag)
    o_rec = sem("o_rec" + tag)
    normed = sem("normed" + tag)
    with ExitStack() as st:
        qop = sb(st, "qop" + tag, [P, BUFS, HG, T], BF16)
        kop = sb(st, "kop" + tag, [P, BUFS, L.key_sets, T], BF16)
        turn = sb(st, "qturn", [P, BUFS, HG, T], BF16) if i == 1 else None
        v_heads = HG if i == 0 else 1
        vst = sb(st, "vst" + tag, [P, BUFS, TB + i, v_heads, 2 * HD], F32)
        prob = sb(st, "prob" + tag, [P, 2, HG, CH], F32)
        wf = sb(st, "wf", [P, KD * E], F32) if i == 1 else None
        negm = sb(st, "negm" + tag, [P, NU], F32)
        mpart = sb(st, "mpart" + tag, [P, 2, P // 2], BF16)
        mrow = sb(st, "mrow" + tag, [P, P], BF16)
        ot = sb(st, "ot" + tag, [P, CH], F32)
        rec = sb(st, "rec" + tag, [P, 2, CT * HG], F32)
        first = plan(L, False, True, False, False)
        start = plan(L, False, True, True, False)
        steady = plan(L, True, True, True, False)
        final = plan(L, True, False, True, True)

        def all_groups(eng, step):
            step(0, 0, start)
            with eng.Fori(0, (N - 2) // BUFS) as turn_:
                for r in range(BUFS):
                    step(turn_ * BUFS + (r + 1), (r + 1) % BUFS, steady)
            step(N - 1, (N - 1) % BUFS, final)

        block = st.enter_context(nc.Block())

        @block.sync
        def _(sp):
            def load(n):
                buf = n % BUFS
                for r in range(NPAIR):
                    rows = slice(R0 + HD * r, R0 + HD * (r + 1))
                    sp.dma_start(qop[rows, buf, :, :].rearrange("p h t -> p (h t)"),
                                 dram.q_parts[i][Q_PART[r], n]).then_inc(loaded[buf], 16)
                    sp.dma_start(kop[rows, buf, :, :].rearrange("p h t -> p (h t)"),
                                 dram.k_parts[i][K_PART[r], n]).then_inc(loaded[buf], 16)
                if i == 1:
                    sp.dma_start(qop[0:NPOS, buf, :, :], dram.qpos[n]).then_inc(loaded[buf], 16)
                    sp.dma_start(turn[0:NPOS, buf, :, :], dram.qturn[n]).then_inc(loaded[buf], 16)

            def send_rows(n):
                sp.wait_ge(m_copied, n + 1)
                for k in range(2):
                    sp.dma_start(qop[RS + k:RS + k + 1, n % BUFS, :, :].rearrange("o h t -> o (h t)"),
                                 mrow[k * P // 2:k * P // 2 + NU, :]).then_inc(m_sent, 16)

            for buf in range(BUFS):
                for v in range(L.key_sets):
                    sp.dma_start(kop[RS:RA, buf, v, :], dram.kpos[NPOS - 2:NPOS, 0, :]).then_inc(const_rows, 16)
                    if i == 1:
                        sp.dma_start(kop[0:NPOS, buf, v, :], dram.kpos[:, v, :]).then_inc(const_rows, 16)
            sp.wait_ge(fills, FILLS)
            load(0)
            load(1)
            send_rows(0)
            load(2)
            for n in range(N - 1):
                if 1 <= n <= N - BUFS:
                    sp.wait_ge(values_done, n * NQ)
                    load(n - 1 + BUFS)
                send_rows(n + 1)

        @block.gpsimd
        def _(pool):
            nc.gpsimd.memset(vst[:], 1.0).then_inc(fills, 1)
            nc.gpsimd.memset(mpart[:], 0.0).then_inc(fills, 1)
            if i == 1:
                nc.gpsimd.memset(turn[:], 0.0).then_inc(fills, 1)
                pool.wait_ge(fills, 3)
                nc.gpsimd.memset(vst[GLOB:P, :, TB, :, :], 0.0).then_inc(fills, 1)
            pool.wait_ge(fills, FILLS)

            def stage(n):
                buf = n % BUFS
                if i == 0:
                    nc.gpsimd.tensor_copy(vst[:, buf, :, :, 0:HD],
                                          K.v_all[:, n, :, :].rearrange("p t (h d) -> p t h d", h=HG)
                                          ).then_inc(v_staged, 1)
                else:
                    nc.gpsimd.tensor_copy(vst[:, buf, 0:TB, 0, 0:HD], K.v_all[:, n, :, :]).then_inc(v_staged, 1)
                    nc.gpsimd.tensor_copy(vst[0:GLOB, buf, TB, 0, 0:HD], K.v_all[0:GLOB, n, TB - 1, :]
                                          ).then_inc(v_staged, 1)

            for n in range(BUFS):
                stage(n)
            for t in range(NT):
                nc.gpsimd.tensor_tensor(K.x[:, t, :], K.x[:, t, :], K.bias[:, i, :], ALU.add).then_inc(residual, 1)
            pool.wait_ge(residual, NT)
            for n in range(N - BUFS):
                if i == 1 and n < 3:
                    if n >= 1:
                        pool.wait_ge(w_cut, 2 * n)
                    wt = dram.ffn[1][n].rearrange("(k p) n -> p k n", p=P)
                    pool.dma_start(wf[:].rearrange("p (k n) -> p k n", k=wt.shape[1]), wt).then_inc(w_loaded, 16)
                    pool.wait_ge(w_loaded, 16 * (n + 1))
                    nc.gpsimd.tensor_copy(K.wffn[:, n, 0, :], wf[:]).then_inc(w_cut, 1)
                    pool.wait_ge(w_cut, 2 * n + 1)
                    nc.gpsimd.tensor_tensor(K.wffn[:, n, 1, :], wf[:], K.wffn[:, n, 0, :].bitcast(F32),
                                            ALU.subtract).then_inc(w_cut, 1)
                pool.wait_ge(values_done, (n + 1) * NQ)
                stage(n + BUFS)

        def score_banks(u):
            return ps[:, S_BANK + 2 * (u % 2):S_BANK + 2 * (u % 2) + 2, :].rearrange("p a c -> p (a c)")

        @block.vector
        def _(dve):
            def step(group, buf, steps):
                for what, k, later in steps:
                    n = group + later
                    if what == "max":
                        lo, hi = maximum_columns(L, k % TB)
                        dve.wait_ge(s_full, n * NU + (k + 1))
                        nc.vector.tensor_reduce(negm[:, k:k + 1], score_banks(k)[:, lo:hi], AX.X, ALU.max,
                                                negate=True).then_inc(max_done, 1)
                    elif what == "rows":
                        dve.wait_ge(max_done, n * NU + NU)
                        nc.vector.tensor_copy(mpart[:, 0, 0:NU], negm[:]).then_inc(m_high, 1)
                        dve.wait_ge(m_high, n + 1)
                        nc.vector.tensor_tensor(mpart[:, 1, 0:NU], negm[:], mpart[:, 0, 0:NU],
                                                ALU.subtract).then_inc(m_cut, 1)
                        dve.wait_ge(m_turned, n + 1)
                        if steps is not first:
                            dve.wait_ge(m_sent, n * 32)
                        nc.vector.tensor_copy(mrow[:], ps[:, SIDE, :].bitcast(BF16)[:, 0:P]).then_inc(m_copied, 1)
                    elif what == "norm":
                        dve.wait_ge(o_turned, n * 2 + (k + 1))
                        if k == 1:
                            dve.wait_ge(normed, n * 2 + 1)
                        side = ps[:, SIDE, :].rearrange("p (a d) -> p a d", d=2 * HD)
                        nc.vector.reciprocal(rec[:, k, :], side[:, :, HD]).then_inc(o_rec, 1)
                        dve.wait_ge(o_rec, n * 2 + (k + 1))
                        nc.vector.tensor_tensor(
                            attn[:, one(n), k * CT:(k + 1) * CT, :].rearrange("p o t (h d) -> p (o t) h d", h=HG),
                            side[:, :, 0:HD].rearrange("p (t h) d -> p t h d", h=HG),
                            rec[:, k, :].rearrange("p (t h) -> p t h", h=HG).unsqueeze(3)
                            .to_broadcast((P, CT, HG, HD)), ALU.mult,
                        ).then_inc(normed, 1)

            step(-1, -1, first)
            all_groups(dve, step)

        @block.scalar
        def _(act):
            def step(group, buf, steps):
                for what, k, later in steps:
                    n = group + later
                    if what == "exp":
                        half, kt = quads[k // HG]
                        lo, hi = columns_of(L, half, kt)
                        rows = key_tile(L, kt)[1]
                        q = k // HG
                        if k % HG == 0 and (q >= 2 or steps is not start):
                            act.wait_ge(values_done, n * NQ + (q - 1))
                        act.wait_ge(t_full, n * NX + (k + 1))
                        nc.scalar.activation(prob[0:rows, q % 2, k % HG, lo % CH:lo % CH + hi - lo],
                                             ps[0:rows, T_BANK + k % 2, lo % CH:lo % CH + hi - lo],
                                             ACT.Exp).then_inc(exp_done, 1)
                    elif what == "evict":
                        act.wait_ge(values_done, n * NQ + (last_quad[k] + 1))
                        if k == 1:
                            act.wait_ge(o_turned, n * 2 + 1)
                        nc.scalar.copy(ot[:], ps[:, O_BANK, :]).then_inc(evicted, 1)

            act.wait_ge(fills, FILLS)
            all_groups(act, step)

        @block.tensor
        def _(pe):
            def score(u, par):
                h, qt = u // TB, u % TB
                i0 = qt * P
                S = score_banks(u)
                q = qop[0:RS, par, h, i0:i0 + P]

                def mm(a, b, lhs, rhs, start):
                    return nc.tensor.matmul(S[:, a:b], lhs, rhs, start=start, stop=True, skip_group_check=True)

                if i == 0:
                    for a, b in cut(0, i0 + P):
                        mm(a, b, q, kop[0:RS, par, h, a:b], True)
                    return mm(i0, i0 + P, identb[:], tri[:, 0, :], False)
                begun = set()
                for what, a, b, off in score_steps(qt):
                    start = a // CH not in begun
                    begun.add(a // CH)
                    if what == "band":
                        last = mm(a, b, identb[:], band[:, off:off + b - a], start)
                    elif what == "turn":
                        last = mm(a, b, turn[0:RS, par, h, i0:i0 + P], kop[0:RS, par, 0, a:b], start)
                    else:
                        last = mm(a, b, q, kop[0:RS, par, 0 if what == "left" else 1, a:b], start)
                return last

            def shifted(k, par):
                half, kt = quads[k // HG]
                h = k % HG
                lo, hi = columns_of(L, half, kt)
                j0, rows = key_tile(L, kt)
                q = qop[0:RA, par, h, :]

                def mm(a, b, lhs, rhs, start):
                    return nc.tensor.matmul(ps[0:rows, T_BANK + k % 2, a % CH:a % CH + b - a], lhs, rhs, start=start,
                                            stop=True, skip_group_check=True)

                if i == 0:
                    last = mm(lo, hi, kop[0:RA, par, h, j0:j0 + P], q[:, lo:hi], True)
                    return mm(j0, j0 + P, identb[:], tri[:, 1, :], False) if lo == j0 else last
                start = True
                for v, a, b in ((1, 0, j0 + WIN), (2, j0 + WIN, j0 + 3 * WIN), (0, j0 + 3 * WIN, T)):
                    a, b = max(a, lo), min(b, hi)
                    if a < b:
                        last = mm(a, b, kop[0:RA, par, v, j0:j0 + rows], q[:, a:b], start)
                        start = False
                a, b = max(j0 - WIN, lo), min(j0 + P + WIN, hi)
                if a < b:
                    off = a - (j0 - WIN)
                    last = mm(a, b, identb[:, 0:rows], band[:, off:off + b - a], False)
                return last

            def values(qd, par):
                half, kt = quads[qd]
                lo, hi = columns_of(L, half, kt)
                vt_ = kt if key_tile(L, kt)[1] == P else TB
                opening = qd == 0 or quads[qd - 1][0] != half
                uniform = opening and i == 1 and half == 0
                if uniform:
                    for t in range(TB):
                        for h in range(HG):
                            nc.tensor.matmul(ps[32 * h:32 * h + 32, O_BANK, 0:GLOB], vst[:, par, t, 0, :],
                                             K.ones[:, 0:GLOB], start=(t == 0), stop=True, skip_group_check=True)
                for h in range(HG):
                    last = nc.tensor.matmul(ps[32 * h:32 * h + 32, O_BANK, lo % CH:lo % CH + hi - lo],
                                            vst[:, par, vt_, h % v_heads, :],
                                            prob[:, qd % 2, h, lo % CH:lo % CH + hi - lo],
                                            start=opening and not uniform, stop=True, skip_group_check=True)
                return last

            def step(group, buf, steps):
                for what, k, later in steps:
                    n = group + later
                    b = (buf + later) % BUFS
                    if what == "max":
                        if k == 0:
                            pe.wait_ge(loaded[b], times_used(n, b) * (16 * group_loads))
                        if steps is not first or k >= 2:
                            pe.wait_ge(max_done, n * NU + (k - 1))
                        score(k, b).then_inc(s_full, 1)
                    elif what == "rows":
                        pe.wait_ge(m_cut, n + 1)
                        if steps is not first:
                            pe.wait_ge(normed, n * 2 - 1)
                        nc.tensor.transpose(ps[:, SIDE, :].bitcast(BF16)[:, 0:P],
                                            mpart[:].rearrange("p k u -> p (k u)"), identb[:]).then_inc(m_turned, 1)
                    elif what == "exp":
                        if k == 0:
                            pe.wait_ge(m_sent, n * 32 + 32)
                            pe.wait_ge(v_staged, (n + 1) * (1 + i))
                        if k >= 2 or steps is not start:
                            pe.wait_ge(exp_done, n * NX + (k - 1))
                        shifted(k, b).then_inc(t_full, 1)
                    elif what == "values":
                        half = quads[k][0]
                        if k > 0 and half != quads[k - 1][0]:
                            pe.wait_ge(evicted, n * 2 + 1)
                        elif k == 0 and steps is not start:
                            pe.wait_ge(evicted, n * 2)
                        pe.wait_ge(exp_done, n * NX + HG * (k + 1))
                        values(k, b).then_inc(values_done, 1)
                    elif what == "norm":
                        pe.wait_ge(evicted, n * 2 + (k + 1))
                        if k == 1 and not (steps is final and later == 0):
                            pe.wait_ge(m_copied, n + 2)
                        elif k == 1 or steps is not start:
                            pe.wait_ge(normed, n * 2 + k)
                        else:
                            pe.wait_ge(m_copied, 1)
                        for j in range(CT):
                            last = nc.tensor.transpose(ps[:, SIDE, j * P:(j + 1) * P], ot[:, j * P:(j + 1) * P],
                                                       ident[:])
                        last.then_inc(o_turned, 1)

            pe.wait_ge(fills, FILLS)
            pe.wait_ge(const_rows, 16 * BUFS * L.key_sets * (1 + i))
            used = [0] * BUFS

            def times_used(n, b):
                return used[b]

            for b in range(BUFS):
                used[b] = 1
            step(-1, -1, first)
            step(0, 0, start)
            with pe.Fori(0, (N - 2) // BUFS) as turn_:
                for r in range(BUFS):
                    used[(r + 2) % BUFS] = turn_ + (1 + (r + 2) // BUFS)
                    step(turn_ * BUFS + (r + 1), (r + 1) % BUFS, steady)
            step(N - 1, (N - 1) % BUFS, final)


def feed_forward(nc, sem, sb, K, L, dram):
    i = L.index
    tag = str(i)
    ps, x, attn, ident = K.ps, K.x, K.attn, K.ident
    last_layer = i == 1
    wo_loaded = sem("wo_loaded" + tag)
    gathered = sem("gathered" + tag)
    a_full = sem("a_full" + tag)
    a_done = sem("a_done" + tag)
    y_full = sem("y_full" + tag)
    y_read = sem("y_read" + tag)
    stat = sem("stat" + tag)
    mean_done = sem("mean_done" + tag)
    rstd = sem("rstd" + tag)
    eps_done = sem("eps_done" + tag)
    normal = sem("normal" + tag)
    n_full = sem("n_full" + tag)
    n_hi = sem("n_hi" + tag)
    n_lo = sem("n_lo" + tag)
    up_full = sem("up_full" + tag)
    gate_full = sem("gate_full" + tag)
    silu_done = sem("silu_done" + tag)
    hid = sem("hid" + tag)
    h_hi = sem("h_hi" + tag)
    h_lo = sem("h_lo" + tag)
    down_full = sem("down_full" + tag)
    stored = sem("stored" + tag)
    pairs = [(0, 0), (0, 1)] if i == 0 else [(0, 0), (0, 1), (1, 0)]
    with ExitStack() as st:
        wo = sb(st, "wo" + tag, [P, KD, D], F32)
        at = sb(st, "at" + tag, [P, KD, CH], F32)
        ag = sb(st, "ag" + tag, [P, 2, CT, D], F32)
        xs = sb(st, "xs" + tag, [P, 2, KD, TOK], F32R)
        hs = sb(st, "hs" + tag, [P, KE, 2, CH], F32R)
        sg = sb(st, "sg" + tag, [P, 2, CH], F32)
        hf = sb(st, "hf" + tag, [P, 2, CH], F32)
        stats = sb(st, "stats" + tag, [P, NT, 6], F32)
        mv = sb(st, "mv" + tag, [P, 2, NT, 2], F32)
        inv = sb(st, "inv" + tag, [P, 2, 2, NT], F32)
        w = K.wffn
        wup = [w[:, 0, s, :].rearrange("p (k n) -> p k n", k=KD) for s in range(1 + i)]
        wgate = [w[:, 1, s, :].rearrange("p (k n) -> p k n", k=KD) for s in range(1 + i)]
        wdown = [w[:, 2, s, :].rearrange("p (k n) -> p k n", k=KE) for s in range(1 + i)]
        out_dst = dram.out.rearrange("(t p) d -> p t d", p=P)
        block = st.enter_context(nc.Block())

        @block.sync
        def _(sp):
            sp.dma_start(wo[:], dram.wo[i].rearrange("(k p) n -> p k n", p=P)).then_inc(wo_loaded, 16)
            if last_layer:
                for c in range(NC):
                    sp.wait_ge(normal, NT + CT * (c + 1))
                    sp.dma_start(out_dst[:, CT * c:CT * c + CT, :], x[:, CT * c:CT * c + CT, :]).then_inc(stored, 16)
                sp.wait_ge(stored, 16 * NC)

        @block.gpsimd
        def _(pool):
            def inverse(c, second):
                tiles = slice(CT * c, CT * c + CT)
                m = c + NC * second
                pool.wait_ge(mean_done, CT * (m + 1))
                nc.gpsimd.tensor_scalar(inv[:, second, 0, tiles], mv[:, second, tiles, 1], LN_EPS, 0.0, ALU.add,
                                        ALU.add).then_inc(eps_done, 1)
                pool.wait_ge(eps_done, m + 1)
                nc.gpsimd.tensor_tensor(inv[:, second, 1, tiles], inv[:, second, 0, tiles], K.power[:],
                                        ALU.pow).then_inc(rstd, 1)

            for c in range(NC):
                inverse(c, 0)
            for c in range(NC):
                for e in range(KE):
                    u = c * KE + e
                    pool.wait_ge(h_hi, u + 1)
                    nc.gpsimd.tensor_tensor(hs[:, e, 1, :], hf[:, u % 2, :], hs[:, e, 0, :].bitcast(F32),
                                            ALU.subtract).then_inc(h_lo, 1)
                    if e == 3 and c >= 1:
                        inverse(c - 1, 1)
            inverse(NC - 1, 1)

        @block.scalar
        def _(act):
            def high(c):
                for k in range(KD):
                    n = c * KD + k
                    act.wait_ge(n_full, n + 1)
                    nc.scalar.copy(xs[:, 0, k, c * CH:(c + 1) * CH], ps[:, 4 + n % 2, :]).then_inc(n_hi, 1)

            for c in range(NC):
                for k in range(KD):
                    n = c * KD + k
                    act.wait_ge(a_full, n + 1)
                    if c >= 1:
                        act.wait_ge(y_full, 2 * c)
                    nc.scalar.copy(at[:, k, :], ps[:, n % 2, :]).then_inc(a_done, 1)
                if c >= 1:
                    high(c - 1)
            high(NC - 1)

            def round_hidden(u):
                c, e = u // KE, u % KE
                act.wait_ge(hid, u + 1)
                if c >= 1 and e == 0:
                    act.wait_ge(down_full, 2 * c)
                nc.scalar.copy(hs[:, e, 0, :], hf[:, u % 2, :]).then_inc(h_hi, 1)

            for u in range(NC * KE):
                act.wait_ge(up_full, u + 1)
                if u >= 2:
                    act.wait_ge(hid, u - 1)
                nc.scalar.activation(sg[:, u % 2, :], ps[:, 2 * (u % 2), :], ACT.Silu,
                                     scale=K.scales[:, 0:1] if i == 0 else 1.0).then_inc(silu_done, 1)
                if u >= 1:
                    round_hidden(u - 1)
            round_hidden(NC * KE - 1)

        @block.vector
        def _(dve):
            def add_and_measure(c, second):
                for hf_ in range(2):
                    t0 = CT * c + 2 * hf_
                    dst = x[:, t0:t0 + 2, :].rearrange("p t d -> p (t d)")
                    if not second:
                        dve.wait_ge(y_full, 2 * c + hf_ + 1)
                        nc.vector.tensor_tensor(dst, ps[:, 2 + hf_, :], dst, ALU.add).then_inc(y_read, 1)
                    else:
                        dve.wait_ge(down_full, 2 * c + hf_ + 1)
                        nc.vector.scalar_tensor_tensor(out=dst, in0=ps[:, 4 + hf_, :],
                                                       scalar=K.scales[:, 2:3] if i == 0 else 1.0, in1=dst,
                                                       op0=ALU.mult, op1=ALU.add).then_inc(y_read, 1)
                m = (c + NC * second)
                for t in range(CT):
                    dve.wait_ge(y_read, 2 * m + t // 2 + 1)
                    nc.vector.bn_stats(stats[:, CT * c + t, :], x[:, CT * c + t, :]).then_inc(stat, 1)
                for t in range(CT):
                    dve.wait_ge(stat, CT * m + t + 1)
                    nc.vector.bn_aggr(mv[:, second, CT * c + t, :], stats[:, CT * c + t, :]).then_inc(mean_done, 1)

            def normalise(c, second):
                m = c + NC * second
                dve.wait_ge(rstd, m + 1)
                dve.wait_ge(mean_done, CT * (m + 1))
                for t in range(CT * c, CT * c + CT):
                    nc.vector.tensor_scalar(x[:, t, :], x[:, t, :], mv[:, second, t, 0:1],
                                            inv[:, second, 1, t:t + 1], ALU.subtract, ALU.mult).then_inc(normal, 1)

            def low(c):
                for k in range(KD):
                    n = c * KD + k
                    dve.wait_ge(n_hi, n + 1)
                    nc.vector.tensor_tensor(xs[:, 1, k, c * CH:(c + 1) * CH], ps[:, 4 + n % 2, :],
                                            xs[:, 0, k, c * CH:(c + 1) * CH].bitcast(F32), ALU.subtract).then_inc(n_lo, 1)

            def gather(c):
                t0 = CT * c % TB
                g0 = (CT * c // TB) * NG
                if c >= 2:
                    dve.wait_ge(a_full, KD * (c - 1))
                nc.vector.tensor_copy(ag[:, c % 2, :, :].rearrange("p t (g d) -> p t g d", g=NG),
                                      attn[:, g0:g0 + NG, t0:t0 + CT, :].rearrange("p g t d -> p t g d")
                                      ).then_inc(gathered, 1)

            gather(0)
            for c in range(NC):
                if c + 1 < NC:
                    gather(c + 1)
                add_and_measure(c, 0)
                if c >= 1:
                    normalise(c - 1, 0)
                if c >= 2:
                    low(c - 2)
            normalise(NC - 1, 0)
            low(NC - 2)
            low(NC - 1)
            for c in range(NC):
                for e in range(KE):
                    u = c * KE + e
                    dve.wait_ge(gate_full, u + 1)
                    dve.wait_ge(silu_done, u + 1)
                    if u >= 2:
                        dve.wait_ge(h_lo, u - 1)
                    nc.vector.scalar_tensor_tensor(out=hf[:, u % 2, :], in0=ps[:, 2 * (u % 2) + 1, :],
                                                   scalar=K.scales[:, 1:2] if i == 0 else 1.0, in1=sg[:, u % 2, :],
                                                   op0=ALU.mult, op1=ALU.mult).then_inc(hid, 1)
                    if c >= 1 and e == 1:
                        add_and_measure(c - 1, 1)
                    if c >= 1 and e == 5:
                        normalise(c - 1, 1)
            add_and_measure(NC - 1, 1)
            normalise(NC - 1, 1)

        @block.tensor
        def _(pe):
            def project_chunk(c):
                pe.wait_ge(gathered, c + 1)
                for k in range(KD):
                    n = c * KD + k
                    if n >= 2:
                        pe.wait_ge(a_done, n - 1)
                    for j in range(CT):
                        last = nc.tensor.transpose(ps[:, n % 2, j * P:(j + 1) * P], ag[:, c % 2, j, k * P:(k + 1) * P],
                                                   ident[:])
                    last.then_inc(a_full, 1)
                pe.wait_ge(a_done, KD * (c + 1))
                for half in range(2):
                    if c >= 1:
                        pe.wait_ge(y_read, 2 * (c - 1) + half + 1)
                    for j in range(2 * half, 2 * half + 2):
                        for k in range(KD):
                            last = nc.tensor.matmul(ps[:, 2 + half, (j % 2) * D:(j % 2 + 1) * D],
                                                    at[:, k, j * P:(j + 1) * P], wo[:, k, :],
                                                    start=(k == 0), stop=(k == KD - 1))
                    last.then_inc(y_full, 1)

            def turn_chunk(c):
                pe.wait_ge(normal, CT * (c + 1))
                for k in range(KD):
                    n = c * KD + k
                    if n >= 2:
                        pe.wait_ge(n_lo, n - 1)
                    for j in range(CT):
                        last = nc.tensor.transpose(ps[:, 4 + n % 2, j * P:(j + 1) * P],
                                                   x[:, CT * c + j, k * P:(k + 1) * P], ident[:])
                    last.then_inc(n_full, 1)

            def unit(u):
                c, e = u // KE, u % KE
                for which, weights, full in ((0, wup, up_full), (1, wgate, gate_full)):
                    if u >= 2:
                        pe.wait_ge(silu_done if which == 0 else hid, u - 1)
                    n = 0
                    for k in range(KD):
                        for a, b in pairs:
                            last = nc.tensor.matmul(ps[:, 2 * (u % 2) + which, :],
                                                    weights[a][:, k, e * P:(e + 1) * P],
                                                    xs[:, b, k, c * CH:(c + 1) * CH],
                                                    start=(n == 0), stop=(n == KD * len(pairs) - 1))
                            n += 1
                    last.then_inc(full, 1)

            def down(c):
                pe.wait_ge(h_lo, KE * (c + 1))
                for half in range(2):
                    if c >= 1:
                        pe.wait_ge(y_read, 2 * NC + 2 * (c - 1) + half + 1)
                    for j in range(2 * half, 2 * half + 2):
                        n = 0
                        for e in range(KE):
                            for a, b in pairs:
                                last = nc.tensor.matmul(ps[:, 4 + half, (j % 2) * D:(j % 2 + 1) * D],
                                                        hs[:, e, b, j * P:(j + 1) * P], wdown[a][:, e, :],
                                                        start=(n == 0), stop=(n == KE * len(pairs) - 1))
                                n += 1
                    last.then_inc(down_full, 1)

            pe.wait_ge(wo_loaded, 16)
            for c in range(NC):
                project_chunk(c)
                if c >= 1:
                    turn_chunk(c - 1)
            turn_chunk(NC - 1)
            pe.wait_ge(n_lo, KD * NC)
            pe.wait_ge(y_read, 2 * NC)
            unit(0)
            unit(1)
            for c in range(NC):
                for u in range(c * KE + 2, min((c + 1) * KE + 2, NC * KE)):
                    unit(u)
                down(c)


def one(n):
    return slice(n, n + 1) if isinstance(n, int) else bass.ds(n, 1)


def build(nc, dram):
    layers = (Layer(0), Layer(1))
    dram.q_parts = [nc.dram_tensor(f"q_parts{i}", (PARTS, N, HD, HG * T), BF16, kind="Internal").ap()
                    for i in range(2)]
    dram.k_parts = [nc.dram_tensor(f"k_parts{i}", (PARTS, N, HD, layers[i].key_sets * T), BF16, kind="Internal").ap()
                    for i in range(2)]
    with ExitStack() as top:
        def sb(stack, name, shape, dt):
            return stack.enter_context(nc.sbuf_tensor(name, shape, dt))

        def sem(name):
            return top.enter_context(nc.semaphore(name))

        K = Chip()
        K.ps = top.enter_context(nc.psum_tensor("ps", [P, 8, CH], F32))
        K.x = sb(top, "x", [P, NT, D], F32)
        K.ident = sb(top, "ident", [P, P], F32)
        K.identb = sb(top, "identb", [P, P], BF16)
        K.tri = sb(top, "tri", [P, 2, P], BF16)
        K.band = sb(top, "band", [P, P + 2 * WIN], BF16)
        K.ones = sb(top, "ones", [P, P], F32)
        K.power = sb(top, "power", [P, CT], F32)
        K.scales = sb(top, "scales", [P, 3], F32)
        K.bias = sb(top, "bias", [P, 2, D], F32)
        for L in layers:
            with ExitStack() as layer:
                K.wffn = sb(layer, f"ffn_parts{L.index}", [P, 3, 1 + L.index, KD * E], F32R)
                K.attn = sb(layer, f"attn{L.index}", [P, N, TB, HG * HD], F32)
                with ExitStack() as values:
                    K.v_all = sb(values, f"v_all{L.index}", [P, N, TB, L.kv_width // NG], F32)
                    project(nc, sem, sb, K, L, dram)
                    attend(nc, sem, sb, K, L, dram)
                feed_forward(nc, sem, sb, K, L, dram)


def bf16_bits(a):
    u = np.ascontiguousarray(a, np.float32).view(np.uint32)
    return ((u + 0x7FFF + ((u >> 16) & 1)) >> 16).astype(np.uint16)


def three_parts(a):
    parts = []
    for _ in range(PARTS):
        p = (bf16_bits(a).astype(np.uint32) << 16).view(np.float32)
        parts.append(p)
        a = a - p
    return parts


def constants():
    r = np.arange(P)
    tri = np.where(r[None, :] > r[:, None], -1e30, 0.0)
    c = np.arange(P + 2 * WIN)
    band = np.where(np.abs(c[None, :] - WIN - r[:, None]) <= WIN, -1e9, 0.0)
    pos = np.arange(T)
    high, low, unit = (pos // P * P).astype(np.float32), (pos % P).astype(np.float32), np.ones(T, np.float32)
    left = np.stack([high] * 3 + [low] * 3 + [unit] * 3)
    mixed = np.where(((pos - GLOB) // GLOB) % 2 == 0, 1.0, -1.0).astype(np.float32)
    kpos = np.stack([left, -left, left * mixed], axis=1)
    slopes = np.float32(2.0 ** (-(2.0 ** -(np.log2(H) - 3.0)))) ** np.arange(1, H + 1, dtype=np.float32)
    s = three_parts(slopes)
    g = three_parts(-(slopes[:, None] * pos[None, :].astype(np.float32)))
    qpos = np.stack([np.broadcast_to(a[:, None], (H, T)) for a in (*s, *s)] + g).astype(np.float32)
    late = (pos % P >= P // 2).astype(np.float32)

    def by_group(a):
        a = a.reshape(NPOS, NG, HG, T).transpose(1, 0, 2, 3)
        return np.concatenate([a] * B)

    return {
        "ident": np.eye(P, dtype=np.float32), "identb": bf16_bits(np.eye(P)),
        "tri": bf16_bits(np.stack([tri, tri.T], axis=1)), "band": bf16_bits(band), "kpos": bf16_bits(kpos),
        "qpos": bf16_bits(by_group(qpos)), "qturn": bf16_bits(by_group(2.0 * qpos * late)),
    }


def kernel(**inputs):
    import concourse.bacc as bacc
    from concourse.bass_utils import run_bass_kernel_spmd as run

    a = {k: np.asarray(v) for k, v in inputs.items()}
    def head_minor(w):
        blocks = [w[:, j:j + D].reshape(D, NG, HG, HD).transpose(0, 1, 3, 2).reshape(D, D)
                  for j in range(0, min(w.shape[1], 2 * D), D)]
        return np.concatenate(blocks + [w[:, 2 * D:]], axis=1)

    arrays = {
        "x": a["L0_attn_x"].reshape(TOK, D),
        "w_qkv0": head_minor(a["L0_attn_w_qkv"]), "w_out0": a["L0_attn_w_out"], "b_out0": a["L0_attn_b_out"].reshape(1, D),
        "up0": a["L0_ffn_W_up"].T, "gate0": a["L0_ffn_W_gate"].T, "down0": a["L0_ffn_W_down"].T,
        "w_q1": head_minor(a["L1_attn_Wq"]), "w_kv1": a["L1_attn_Wkv"], "w_out1": a["L1_attn_Wo"],
        "b_out1": a["L1_attn_bo"].reshape(1, D),
        "gate1": a["L1_ffn_w_gate"].T, "up1": a["L1_ffn_w_up"].T, "down1": a["L1_ffn_w_down"].T,
        **constants(),
    }
    arrays = {k: np.ascontiguousarray(v) for k, v in arrays.items()}
    nc = bacc.Bacc("TRN2", target_bir_lowering=False, num_devices=1)
    t = {k: nc.dram_tensor("in_" + k, v.shape, mybir.dt.from_np(v.dtype), kind="ExternalInput").ap()
         for k, v in arrays.items()}
    t = {k: v.bitcast(BF16) if v.dtype == mybir.dt.uint16 else v for k, v in t.items()}
    out = nc.dram_tensor("out", (TOK, D), F32, kind="ExternalOutput").ap()
    dram = Dram()
    dram.x, dram.out = t["x"], out
    dram.ident, dram.identb, dram.tri, dram.band = t["ident"], t["identb"], t["tri"], t["band"]
    dram.kpos, dram.qpos, dram.qturn = t["kpos"], t["qpos"], t["qturn"]
    dram.wq, dram.wkv = (t["w_qkv0"], t["w_q1"]), t["w_kv1"]
    dram.wo, dram.bias = (t["w_out0"], t["w_out1"]), (t["b_out0"], t["b_out1"])
    dram.ffn = ((t["up0"], t["gate0"], t["down0"]), (t["gate1"], t["up1"], t["down1"]))
    build(nc, dram)
    r = run(nc, [{"in_" + k: v for k, v in arrays.items()}], core_ids=[0])
    return r.results[0]["out"].reshape(B, T, D)
```

```python
from contextlib import ExitStack

import numpy as np
import concourse.bass as bass
from concourse import mybir

ALU = mybir.AluOpType
ACT = mybir.ActivationFunctionType
AX = mybir.AxisListType
F32 = mybir.dt.float32
F32R = mybir.dt.float32r
BF16 = mybir.dt.bfloat16

P = 128
B, T, D = 2, 1024, 256
TOK = B * T
NT = TOK // P
TB = T // P
KD = D // P
H, HD = 16, 16
HG = 4
NG = H // HG
N = B * NG
E = 1024
KE = E // P
CH = 512
NC = TOK // CH
RING = 4
CT = CH // P
WIN, GLOB = 32, 64
PARTS = 3
Q_PART = (0, 0, 0, 1, 1, 2)
K_PART = (0, 1, 2, 0, 1, 0)
NPAIR = len(Q_PART)
BUFS = 3
KEY_TILES_AHEAD = (4, 3)
NPOS = 9
LN_EPS = 1e-5
QUANT_EPS = 1e-8


class Chip:
    pass


class Dram:
    pass


class Layer:

    def __init__(self, index):
        self.index = index
        self.first_row = 0 if index == 0 else NPOS
        self.score_rows = self.first_row + NPAIR * HD
        self.rows = self.score_rows + 2
        self.key_sets = HG if index == 0 else 3
        self.kv_width = D if index == 0 else D // HG


def maximum_columns(layer, qt):
    return (0, (qt + 1) * P) if layer.index == 0 else (GLOB, T)


def cut(lo, hi):
    return [(a, min(b, hi)) for a, b in ((max(lo, c), c + CH) for c in range(0, T, CH)) if a < min(b, hi)]


def score_steps(qt):
    i0 = qt * P
    turn = max(GLOB, i0 + WIN)
    steps = [("left", a, b, 0) for a, b in cut(GLOB, turn)]
    steps += [("right", a, b, 0) for a, b in cut(turn, T)]
    steps += [("turn", a, b, 0) for a, b in cut(turn, i0 + 3 * WIN)]
    steps += [("band", a, b, a - (i0 - WIN)) for a, b in cut(max(GLOB, i0 - WIN), min(T, i0 + P + WIN))]
    return sorted(steps, key=lambda s: s[1] // CH)


def units_of(layer):
    return [(h, qt, a, b) for h in range(HG) for qt in range(TB) for a, b in cut(*maximum_columns(layer, qt))]


def key_tile(layer, kt):
    if layer.index == 0:
        return kt * P, P
    j0 = GLOB + kt * P
    return j0, min(P, T - j0)


def columns_of(layer, half, kt):
    lo, hi = half * CH, (half + 1) * CH
    return (max(lo, kt * P), hi) if layer.index == 0 else (max(lo, GLOB), hi)


def quads_of(layer):
    return [(half, kt) for half in range(2) for kt in range(TB)
            if columns_of(layer, half, kt)[0] < columns_of(layer, half, kt)[1]]


def selected(layer, half, kt):
    lo, hi = columns_of(layer, half, kt)
    return kt * P if layer.index == 0 and lo <= kt * P < hi else None


def plan(layer, late, scores, values, ends):
    units = list(range(len(units_of(layer)))) if scores else []
    if not values:
        return [("max", u, 1) for u in units] + [("rows", 0, 1)]
    quads = quads_of(layer)
    nq = len(quads)
    steps, given = [], 0
    tail = [("values", nq - 1), ("evict", 1), ("norm", 1)]
    rows_at = nq - KEY_TILES_AHEAD[layer.index]
    for n, (half, kt) in enumerate(quads):
        due = min(len(units), -(-len(units) * (n + 1) // rows_at))
        for h in range(HG):
            steps.append(("exp", HG * n + h, 0))
            upto = given + -(-(due - given) // (HG - h))
            steps += [("max", u, 1) for u in units[given:upto]]
            given = upto
        if n == 0 and late:
            steps += [(what, k, -1) for what, k in tail[:2]]
        if n == 1 and late:
            steps.append((*tail[2], -1))
        if n == 1 and scores:
            steps.append(("stage", 0, 1))
        if scores and not late and layer.index == 1:
            steps += [("cut", k, 0) for k, at in enumerate((2, 3, 7, 8, 11, 12)) if at == n]
        if n >= 1:
            steps.append(("values", n - 1, 0))
            if quads[n - 1][0] != half:
                steps.append(("evict", quads[n - 1][0], 0))
        if n >= 2 and quads[n - 2][0] != quads[n - 1][0]:
            steps.append(("norm", quads[n - 2][0], 0))
        if units and n == rows_at:
            steps.append(("rows", 0, 1))
    if ends:
        steps += [(what, k, 0) for what, k in tail]
    return steps


def with_preparation(steps, nq):
    at = {2: [("gather", 0), ("turn_attn", 0), ("copy_attn", 0), ("gather", 1)],
          4: [("project", 0), ("add", 0), ("turn_attn", 1), ("copy_attn", 1)],
          5: [("inverse", 0)],
          6: [("project", 1), ("add", 1), ("normalise", 0)],
          7: [("inverse", 1)],
          8: [("turn_x", 0), ("high", 0), ("low", 0), ("normalise", 1)],
          10: [("turn_x", 1), ("high", 1), ("low", 1)]}
    out = []
    for step in steps:
        out.append(step)
        if step[0] == "values" and step[2] == 0:
            out += [(what, c, 0) for what, c in at.get(step[1], ())]
    return out


def project(nc, sem, sb, K, L, dram, prep):
    i = L.index
    tag = str(i)
    ps, x, ident = K.ps, K.x, K.ident
    x_loaded = [sem(f"x_loaded{c}") for c in range(NC)] if i == 0 else None
    ident_loaded = sem("ident_loaded") if i == 0 else None
    const_loaded = sem("const_loaded") if i == 0 else None
    w_loaded = sem("wqkv_loaded" + tag)
    ffn_loaded = sem("ffn_loaded0") if i == 0 else None
    xt_full = sem("xt_full" + tag)
    xt_act = sem("xt_act" + tag)
    xt_dve = sem("xt_dve" + tag)
    proj_full = sem("proj_full" + tag)
    part1 = sem("part1_done" + tag)
    rest1 = sem("rest1_done" + tag)
    part2 = sem("part2_done" + tag)
    part3 = sem("part3_done" + tag)
    operands = K.operands
    sent = operands.sent
    v_full = sem("v_full" + tag)
    v_done = sem("v_done" + tag)
    vt_done = sem("vt_done" + tag)
    cw_step = sem("cw_step" + tag)
    xc_ready = sem("xc_ready" + tag)
    ones_set = sem("ones_set" + tag)
    abs_sum = sem("abs_sum" + tag)
    total = sem("abs_total" + tag)
    tern = sem("ternary_step" + tag)

    NW = 3 * D if i == 0 else D + 2 * L.kv_width
    with ExitStack() as st:
        xt = K.attn[:].rearrange("p n t d -> p (n t d)").rearrange("p (k t) -> p k t", k=KD)
        w = sb(st, "wqkv" + tag, [P, KD, NW], F32)
        part = [buf[:, BUFS - 1, :, :].rearrange("p h t -> p (h t)")[:, j * PARTS * CH:(j + 1) * PARTS * CH]
                .rearrange("p (k c) -> p k c", k=PARTS) for buf in (K.qop, K.kop) for j in range(RING // 2)]
        rest = K.staging[:].rearrange("p (r c) -> p r c", r=RING)
        if i == 0:
            wf = sb(st, "wffn", [P, 3, KD * E], F32)
            wsum = sb(st, "wsum", [P, 3], F32)
            thr = sb(st, "thr", [P, 2, 3], F32)
            below = prep.xs[:].rearrange("p r s k c -> p (r s k c)")[:, 0:KD * E]
            units = [(b, m, c) for b in range(B) for m in range(2 * KD) for c in range(2)]
            v_units = [(b, c) for b in range(B) for c in range(TB // 2)]
        else:
            xct = sb(st, "xct", [P, KD, TOK], F32)
            xc = sb(st, "xc", [P, CT, D], F32)
            vt = sb(st, "vt", [P, B, T + GLOB], F32)
            cw = sb(st, "cw", [P, 4, NT], F32)
            units = [(b, m, c) for b in range(B) for m in (KD, 0, 1) for c in range(2)]
            v_units = list(range(B))
        turns = [(c, s, k) for c in range(NC) for s in range(1 + i) for k in range(KD)]

        def is_q(m):
            return m < KD

        def rows_of(m):
            return P if i == 0 or is_q(m) else L.kv_width

        def sent_before(u, k):
            return len(range(k, u, RING))

        K.parts_in_dram = [16 * sent_before(len(units), k) for k in range(RING)]
        half_way = len(units) // 2

        if i == 0:
            order = [o for u in range(0, len(units), 2) for o in (("qk", u), ("qk", u + 1), ("v", u // 2))]
        else:
            order = [("qk", u) for u in range(len(units))]
            order[4:4] = [("v", 0)]
            order += [("v", 1)]
        block = st.enter_context(nc.Block())

        @block.sync
        def _(sp):
            if i == 1:
                operands.constants(sp, 0)
                operands.constants(sp, 1)
            else:
                xv = dram.x.rearrange("(t p) d -> p t d", p=P)
                sp.dma_start(ident[:], dram.ident).then_inc(ident_loaded, 16)
                for c in range(NC):
                    sp.dma_start(x[:, CT * c:CT * c + CT, :], xv[:, CT * c:CT * c + CT, :]).then_inc(x_loaded[c], 16)
                operands.constants(sp, 0)
                operands.constants(sp, 1)
            for u, (b, m, c) in enumerate(units):
                if u == half_way + 2:
                    for k in range(RING):
                        sp.wait_ge(sent[k], 16 * sent_before(half_way, k))
                    operands.load(sp, 0)
                sp.wait_ge(part3, u + 1)
                sp.wait_ge(part2, u + 1)
                r = rows_of(m)
                cols = slice(c * CH, (c + 1) * CH)
                if i == 0 or is_q(m):
                    g0 = b * NG + (m % KD) * (NG // KD)
                    dst = (dram.q_parts if is_q(m) else dram.k_parts)[i][:, g0:g0 + NG // KD]
                    dst = dst.rearrange("k g d (h t) -> (g d h) k t", t=T)[:, :, cols]
                    sp.dma_start(dst, part[u % RING][0:r, :, :]).then_inc(sent[u % RING], 16)
                else:
                    dst = dram.k_parts[i][:, b * NG:(b + 1) * NG].rearrange("k g d t -> (g d) k t")[:, :, cols]
                    sp.dma_start(dst, part[u % RING][0:r, :, :]).then_inc(sent[u % RING], 16)

        if i == 0:
            @block.gpsimd
            def _(pool):
                nc.gpsimd.memset(K.ones[:], 1.0).then_inc(ones_set, 1)
                nc.gpsimd.memset(K.power[:], -0.5).then_inc(ones_set, 1)
                pool.wait_ge(x_loaded[NC - 1], 16)
                for j, wt in enumerate(dram.ffn[0]):
                    wt = wt.rearrange("(k p) n -> p k n", p=P)
                    pool.dma_start(wf[:, j, :].rearrange("p (k n) -> p k n", k=wt.shape[1]), wt
                                   ).then_inc(ffn_loaded, 16)
                pool.dma_start(K.identb[:], dram.identb).then_inc(const_loaded, 16)
                pool.dma_start(K.tri[:], dram.tri).then_inc(const_loaded, 16)
                pool.dma_start(K.band[:], dram.band).then_inc(const_loaded, 16)
                for j in range(2):
                    pool.dma_start(K.bias[:, j, :], dram.bias[j].to_broadcast((P, D))).then_inc(const_loaded, 16)
                pool.wait_ge(const_loaded, 16 * 5)

        @block.scalar
        def _(act):
            if i == 0:
                act.dma_start(w[:], dram.wq[0].rearrange("(k p) n -> p k n", p=P)).then_inc(w_loaded, 16)
            else:
                act.dma_start(w[:, :, 0:D], dram.wq[1].rearrange("(k p) n -> p k n", p=P)).then_inc(w_loaded, 16)
                act.dma_start(w[:, :, D:NW], dram.wkv.rearrange("(k p) n -> p k n", p=P)).then_inc(w_loaded, 16)
                act.wait_ge(cw_step, 1)
                nc.scalar.activation(cw[:, 1, :], cw[:, 0, :], ACT.Exp, scale=-1.0).then_inc(cw_step, 1)
            for n, (c, s, k) in enumerate(turns):
                if k == 0:
                    act.wait_ge(xt_full, n + 1)
                    dst = xct if s else xt
                    nc.scalar.copy(dst[:, k, c * CH:(c + 1) * CH], ps[:, n % 2, :]).then_inc(xt_act, 1)

            def second_part(u):
                r = rows_of(units[u][1])
                act.wait_ge(rest1, u + 1)
                nc.scalar.copy(part[u % RING][0:r, 1, :], rest[0:r, u % RING, :]).then_inc(part2, 1)

            for what, u in order:
                if what == "v":
                    act.wait_ge(v_full, u + 1)
                    if i == 0:
                        b, c = v_units[u]
                        for j in range(2):
                            nc.scalar.copy(K.v_all[:, b * NG:(b + 1) * NG, 2 * c + j, :],
                                           ps[:, 6 + u % 2, j * D:(j + 1) * D].rearrange("p (g d) -> p g d", g=NG)
                                           ).then_inc(v_done, 1)
                    else:
                        nc.scalar.copy(K.v_all[:, u * NG:(u + 1) * NG, :, :],
                                       ps[:, 6 + u, :].rearrange("p (t g d) -> p g t d", t=TB, g=NG)
                                       ).then_inc(v_done, 1)
                    continue
                b, m, c = units[u]
                r = rows_of(m)
                act.wait_ge(proj_full, u + 1)
                if u >= RING:
                    act.wait_ge(sent[u % RING], 16 * sent_before(u, u % RING))
                nc.scalar.activation(part[u % RING][0:r, 0, :], ps[0:r, 2 + u % 4, :], ACT.Copy,
                                     scale=0.25 if is_q(m) else 1.0).then_inc(part1, 1)
                if i == 1 and not is_q(m):
                    nc.scalar.copy(vt[r:P, b, c * CH:(c + 1) * CH], ps[r:P, 2 + u % 4, :]).then_inc(vt_done, 1)
                    if c == 0:
                        nc.scalar.copy(vt[r:P, b, T:T + GLOB], ps[r:P, 2 + u % 4, 0:GLOB]).then_inc(vt_done, 1)
                if u >= 1:
                    second_part(u - 1)
            second_part(len(units) - 1)

        @block.vector
        def _(dve):
            if i == 1:
                nc.vector.tensor_reduce(cw[:, 0, :], x[:], AX.X, ALU.add,
                                        apply_absolute_value=True).then_inc(cw_step, 1)
                dve.wait_ge(cw_step, 2)
                nc.vector.tensor_scalar(cw[:, 2, :], cw[:, 1, :], 1.0, None, ALU.add).then_inc(cw_step, 1)
                dve.wait_ge(cw_step, 3)
                nc.vector.reciprocal(cw[:, 3, :], cw[:, 2, :]).then_inc(cw_step, 1)
                dve.wait_ge(cw_step, 4)

            def scaled(c):
                if c >= 1:
                    dve.wait_ge(xt_full, turns.index((c - 1, 1, 1)) + 1)
                for t in range(CT):
                    nc.vector.tensor_scalar(xc[:, t, :], x[:, CT * c + t, :], cw[:, 3, CT * c + t:CT * c + t + 1],
                                            None, ALU.mult).then_inc(xc_ready, 1)

            for n, (c, s, k) in enumerate(turns):
                if i == 1 and s == 0 and k == 0:
                    scaled(c)
                if k == 1:
                    dve.wait_ge(xt_full, n + 1)
                    dst = xct if s else xt
                    nc.vector.tensor_copy(dst[:, k, c * CH:(c + 1) * CH], ps[:, n % 2, :]).then_inc(xt_dve, 1)

            def third_part(u):
                r = rows_of(units[u][1])
                dve.wait_ge(part2, u + 1)
                nc.vector.tensor_tensor(part[u % RING][0:r, 2, :], rest[0:r, u % RING, :], part[u % RING][0:r, 1, :],
                                        ALU.subtract).then_inc(part3, 1)

            def ternary(piece):
                if piece < 3:
                    j = piece
                    dve.wait_ge(ffn_loaded, 16 * 3)
                    nc.vector.tensor_reduce(wsum[:, j:j + 1], wf[:, j, :], AX.X, ALU.add,
                                            apply_absolute_value=True).then_inc(abs_sum, 1)
                elif piece == 3:
                    dve.wait_ge(total, 1)
                    nc.vector.tensor_scalar(K.scales[:], ps[:, 0, 0:3], 1.0 / (D * E), QUANT_EPS, ALU.mult,
                                            ALU.add).then_inc(tern, 1)
                    dve.wait_ge(tern, 1)
                    for s in range(2):
                        nc.vector.tensor_scalar(thr[:, s, :], K.scales[:], 0.5 - s, None, ALU.mult).then_inc(tern, 1)
                else:
                    j = piece - 4
                    dve.wait_ge(tern, 3 + 2 * j)
                    nc.vector.tensor_scalar(below, wf[:, j, :], thr[:, 1, j:j + 1], None, ALU.is_lt).then_inc(tern, 1)
                    dve.wait_ge(tern, 4 + 2 * j)
                    nc.vector.scalar_tensor_tensor(out=K.wffn[:, j, 0, :], in0=wf[:, j, :], scalar=thr[:, 0, j:j + 1],
                                                   in1=below.bitcast(F32), op0=ALU.is_gt, op1=ALU.subtract).then_inc(tern, 1)

            for what, u in order:
                if what == "v":
                    if i == 0 and u >= 1:
                        ternary(u - 1)
                    continue
                b, m, c = units[u]
                r = rows_of(m)
                dve.wait_ge(part1, u + 1)
                if u >= RING:
                    dve.wait_ge(part3, u - RING + 1)
                nc.vector.scalar_tensor_tensor(
                    out=rest[0:r, u % RING, :], in0=ps[0:r, 2 + u % 4, :], scalar=0.25 if is_q(m) else 1.0,
                    in1=part[u % RING][0:r, 0, :], op0=ALU.mult, op1=ALU.subtract).then_inc(rest1, 1)
                if u >= 1:
                    third_part(u - 1)
            third_part(len(units) - 1)

        @block.tensor
        def _(pe):
            if i == 0:
                pe.wait_ge(ident_loaded, 16)
            for n, (c, s, k) in enumerate(turns):
                if i == 0 and k == 0:
                    pe.wait_ge(x_loaded[c], 16)
                if s == 1 and k == 0:
                    pe.wait_ge(xc_ready, CT * (c + 1))
                if n >= 2:
                    pe.wait_ge(xt_act if k == 0 else xt_dve, (n - 2) // 2 + 1)
                for j in range(CT):
                    src = xc[:, j, k * P:(k + 1) * P] if s else x[:, CT * c + j, k * P:(k + 1) * P]
                    last = nc.tensor.transpose(ps[:, n % 2, j * P:(j + 1) * P], src, ident[:])
                last.then_inc(xt_full, 1)
            pe.wait_ge(xt_act, len(turns) // 2)
            pe.wait_ge(xt_dve, len(turns) // 2)
            pe.wait_ge(w_loaded, 16 * (1 + i))
            for what, u in order:
                if what == "v":
                    if i == 0:
                        b, c = v_units[u]
                        if u >= 2:
                            pe.wait_ge(v_done, 2 * (u - 1))
                        for j in range(2):
                            t0 = b * T + (2 * c + j) * P
                            for k in range(KD):
                                last = nc.tensor.matmul(ps[:, 6 + u % 2, j * D:(j + 1) * D], xt[:, k, t0:t0 + P],
                                                        w[:, k, 2 * D:3 * D], start=(k == 0), stop=(k == KD - 1))
                        if u == 3:
                            pe.wait_ge(abs_sum, 3)
                            pe.wait_ge(ones_set, 1)
                            nc.tensor.matmul(ps[:, 0, 0:3], K.ones[:], wsum[:], start=True, stop=True
                                             ).then_inc(total, 1)
                    else:
                        pe.wait_ge(vt_done, 3 * (u + 1))
                        for t in range(TB):
                            j0 = GLOB + t * P
                            last = nc.tensor.transpose(ps[:, 6 + u, t * HG * HD:(t + 1) * HG * HD],
                                                       vt[L.kv_width:P, u, j0:j0 + P],
                                                       ident[L.kv_width:P, L.kv_width:P])
                    last.then_inc(v_full, 1)
                    continue
                b, m, c = units[u]
                if u >= 4:
                    pe.wait_ge(rest1, u - 3)
                    copies = sum((2 if cc == 0 else 1) for (_, mm, cc) in units[:u - 3] if mm == KD) if i else 0
                    if copies:
                        pe.wait_ge(vt_done, copies)
                src = xct if i == 1 and is_q(m) else xt
                t0 = b * T + c * CH
                for k in range(KD):
                    last = nc.tensor.matmul(ps[:, 2 + u % 4, :], w[:, k, m * P:(m + 1) * P],
                                            src[:, k, t0:t0 + CH], start=(k == 0), stop=(k == KD - 1))
                last.then_inc(proj_full, 1)


class Operands:

    def __init__(self, nc, sem, K, L, dram):
        tag = str(L.index)
        self.K, self.L, self.dram = K, L, dram
        self.loaded = [sem(f"operands_loaded{tag}{k}") for k in range(BUFS)]
        self.const_rows = [sem(f"constant_rows{tag}{k}") for k in range(2)]
        self.sent = [sem(f"parts_sent{tag}{k}") for k in range(RING)]
        self.loads = 2 * NPAIR + L.index
        self.consts = 1 + L.index

    def constants(self, sp, buf):
        L, kop, kpos = self.L, self.K.kop, self.dram.kpos
        sp.dma_start(kop[L.score_rows:L.rows, buf, :, :],
                     kpos[NPOS - 2:NPOS, 0:1, :].to_broadcast((2, L.key_sets, T))).then_inc(self.const_rows[buf // (BUFS - 1)], 16)
        if L.index == 1:
            sp.dma_start(kop[0:NPOS, buf, :, :], kpos).then_inc(self.const_rows[buf // (BUFS - 1)], 16)

    def load(self, sp, n):
        L, qop, kop, buf = self.L, self.K.qop, self.K.kop, n % BUFS
        for r in range(NPAIR):
            rows = slice(L.first_row + HD * r, L.first_row + HD * (r + 1))
            sp.dma_start(qop[rows, buf, :, :].rearrange("p h t -> p (h t)"),
                         self.dram.q_parts[L.index][Q_PART[r], n]).then_inc(self.loaded[buf], 16)
            k = self.dram.k_parts[L.index][K_PART[r], n]
            sp.dma_start(kop[rows, buf, :, :],
                         k.rearrange("d (h t) -> d h t", t=T) if L.index == 0
                         else k.unsqueeze(1).to_broadcast((HD, L.key_sets, T))).then_inc(self.loaded[buf], 16)
        if L.index == 1:
            sp.dma_start(qop[0:NPOS, buf, :, :], self.dram.qpos[n]).then_inc(self.loaded[buf], 16)


def attend(nc, sem, sb, K, L, dram, prep):
    i = L.index
    tag = str(i)
    ps, attn, ident, identb, tri, band = K.ps, K.attn, K.ident, K.identb, K.tri, K.band
    R0, RS, RA = L.first_row, L.score_rows, L.rows
    quads = quads_of(L)
    units = units_of(L)
    NU, NX, NQ = len(units), HG * len(quads), len(quads)
    NM = HG * TB
    two_from = 0 if i == 1 else TB // 2
    last_quad = [max(q for q in range(NQ) if quads[q][0] == half) for half in range(2)]
    operands, qop, kop = K.operands, K.qop, K.kop
    loaded = operands.loaded
    S_SLOTS = 4
    S_BANK, T_BANK, O_BANK, SIDE = 0, 4, 6, 7
    turn_loaded = sem("turning_operand_loaded") if i == 1 else None
    fills = sem("constants_filled" + tag)
    FILLS = 2 + 2 * i
    v_staged = sem("v_staged" + tag)
    residual = prep.residual
    s_full = sem("s_full" + tag)
    max_done = sem("max_done" + tag)
    m_high = sem("m_high" + tag)
    m_cut = sem("m_cut" + tag)
    m_turned = sem("m_turned" + tag)
    m_copied = sem("m_copied" + tag)
    m_sent = sem("m_sent" + tag)
    w_loaded = sem("ffn_loaded1") if i == 1 else None
    diagonal = [selected(L, *quad) for quad in quads]
    upto = [sum(d is not None for d in diagonal[:q + 1]) for q in range(len(quads))]
    w_cut = sem("ffn_weights_cut") if i == 1 else None
    t_full = sem("t_full" + tag)
    exp_done = sem("exp_done" + tag)
    masked = sem("masked" + tag)
    values_done = sem("values_done" + tag)
    evicted = sem("evicted" + tag)
    o_turned = sem("o_turned" + tag)
    o_rec = sem("o_rec" + tag)
    normed = prep.normed
    with ExitStack() as st:
        turn = sb(st, "qturn", [P, HG, T], BF16) if i == 1 else None
        v_heads = HG if i == 0 else 1
        vst = sb(st, "vst" + tag, [P, BUFS, TB + i, v_heads, 2 * HD], F32)
        prob = sb(st, "prob" + tag, [P, 2, HG, CH], F32)
        wf = K.staging
        negm = sb(st, "negm" + tag, [P, 2, HG, TB], F32)
        mpart = sb(st, "mpart" + tag, [P, 2, P // 2], BF16)
        mrow = sb(st, "mrow" + tag, [P, P], BF16)
        ot = sb(st, "ot" + tag, [P, CH], F32)
        rec = sb(st, "rec" + tag, [P, 2, CT * HG], F32)
        first = plan(L, False, True, False, False)
        start = plan(L, False, True, True, False)
        steady = plan(L, True, True, True, False)
        final = with_preparation(plan(L, True, False, True, True), NQ)

        def all_groups(eng, step):
            step(0, 0, start)
            with eng.Fori(0, (N - 2) // BUFS) as turn_:
                for r in range(BUFS):
                    step(turn_ * BUFS + (r + 1), (r + 1) % BUFS, steady)
            step(N - 1, (N - 1) % BUFS, final)

        block = st.enter_context(nc.Block())

        @block.sync
        def _(sp):
            def load_turn(n):
                sp.dma_start(turn[0:NPOS, :, :], dram.qturn[n]).then_inc(turn_loaded, 16)

            def send_rows(n):
                sp.wait_ge(m_copied, n + 1)
                if i == 1 and n + 1 < N:
                    load_turn(n + 1)
                for k in range(2):
                    sp.dma_start(qop[RS + k:RS + k + 1, n % BUFS, :, :].rearrange("o h t -> o (h t)"),
                                 mrow[k * P // 2:k * P // 2 + NM, :]).then_inc(m_sent, 16)

            if i == 1:
                sp.wait_ge(fills, 1)
                load_turn(0)
            operands.load(sp, 1)
            for k in range(RING):
                sp.wait_ge(operands.sent[k], K.parts_in_dram[k])
            operands.constants(sp, BUFS - 1)
            operands.load(sp, BUFS - 1)
            sp.dma_start(prep.wo[:], dram.wo[i].rearrange("(k p) n -> p k n", p=P)).then_inc(prep.wo_loaded, 16)
            send_rows(0)
            for j in range(3 if i == 1 else 0):
                if j >= 1:
                    sp.wait_ge(w_cut, 4 * j)
                wt = dram.ffn[1][j].rearrange("(k p) n -> p k n", p=P)
                sp.dma_start(wf[:].rearrange("p (k n) -> p k n", k=wt.shape[1]), wt).then_inc(w_loaded, 16)
            for n in range(N - 1):
                if 1 <= n <= N - BUFS:
                    sp.wait_ge(values_done, n * NQ)
                    operands.load(sp, n - 1 + BUFS)
                send_rows(n + 1)

        @block.gpsimd
        def _(pool):
            if i == 1:
                nc.gpsimd.memset(turn[:], 0.0).then_inc(fills, 1)
                pool.wait_ge(fills, 1)
            nc.gpsimd.memset(mpart[:], 0.0).then_inc(fills, 1)
            nc.gpsimd.memset(vst[:], 1.0).then_inc(fills, 1)
            if i == 1:
                pool.wait_ge(fills, 3)
                nc.gpsimd.memset(vst[GLOB:P, :, TB, :, :], 0.0).then_inc(fills, 1)
            pool.wait_ge(fills, FILLS)

            def stage(n, buf):
                if i == 0:
                    nc.gpsimd.tensor_copy(vst[:, buf, :, :, 0:HD],
                                          K.v_all[:, one(n), :, :].rearrange("p o t (h d) -> p (o t) h d", h=HG)
                                          ).then_inc(v_staged, 1)
                else:
                    nc.gpsimd.tensor_copy(vst[:, buf, 0:TB, 0, 0:HD],
                                          K.v_all[:, one(n), :, :].rearrange("p o t d -> p (o t) d")
                                          ).then_inc(v_staged, 1)
                    nc.gpsimd.tensor_copy(vst[0:GLOB, buf, TB:TB + 1, 0, 0:HD], K.v_all[0:GLOB, one(n), TB - 1, :]
                                          ).then_inc(v_staged, 1)

            def step(group, buf, steps):
                for what, k, later in steps:
                    n = group + later
                    if what == "exp" and k % HG == HG - 1 and diagonal[k // HG] is not None:
                        pool.wait_ge(exp_done, n * NX + (k + 1))
                        a = diagonal[k // HG] % CH
                        cells = prob[:, k // HG % 2, :, a:a + P]
                        nc.gpsimd.affine_select(out=cells, in_=cells, pattern=[[0, HG], [1, P]],
                                                compare_op=ALU.is_ge, fill=zero, base=0, channel_multiplier=-1
                                                ).then_inc(masked, 1)
                    elif what == "stage":
                        if steps is not start:
                            pool.wait_ge(values_done, group * NQ)
                        stage(n, (buf + 1) % BUFS)
                    elif what == "cut":
                        j, cols = k // 2, slice(k % 2 * E, (k % 2 + 1) * E)
                        pool.wait_ge(w_loaded, 16 * (j + 1))
                        nc.gpsimd.tensor_copy(K.wffn[:, j, 0, cols], wf[:, cols]).then_inc(w_cut, 1)
                        pool.wait_ge(w_cut, 2 * k + 1)
                        nc.gpsimd.tensor_tensor(K.wffn[:, j, 1, cols], wf[:, cols],
                                                K.wffn[:, j, 0, cols].bitcast(F32), ALU.subtract).then_inc(w_cut, 1)
                    elif what == "inverse":
                        prep.inverse(pool, k, 0)

            zero = nc.gpsimd.to_reg(0.0) if i == 0 else None
            stage(0, 0)
            for t in range(NT):
                nc.gpsimd.tensor_tensor(K.x[:, t, :], K.x[:, t, :], K.bias[:, i, :], ALU.add).then_inc(residual, 1)
            pool.wait_ge(residual, NT)
            step(0, 0, start)
            for n in range(1, N - 1):
                step(n, n % BUFS, steady)
            step(N - 1, (N - 1) % BUFS, final)

        @block.vector
        def _(dve):
            def step(group, buf, steps):
                for what, k, later in steps:
                    n = group + later
                    if what == "max":
                        h, qt, lo, hi = units[k]
                        dve.wait_ge(s_full, n * NU + (k + 1))
                        nc.vector.tensor_reduce(negm[:, lo // CH, h, qt:qt + 1],
                                                ps[:, S_BANK + k % S_SLOTS, lo % CH:lo % CH + hi - lo], AX.X, ALU.max,
                                                negate=True).then_inc(max_done, 1)
                    elif what == "rows":
                        dve.wait_ge(max_done, n * NU + NU)
                        if steps is first:
                            dve.wait_ge(fills, FILLS)
                        both = negm[:, :, :, two_from:TB]
                        nc.vector.tensor_tensor(both[:, 0], both[:, 0], both[:, 1], ALU.min).then_inc(m_high, 1)
                        dve.wait_ge(m_high, n * 2 + 1)
                        whole = negm[:, 0].rearrange("p h t -> p (h t)")
                        nc.vector.tensor_copy(mpart[:, 0, 0:NM], whole).then_inc(m_high, 1)
                        dve.wait_ge(m_high, n * 2 + 2)
                        nc.vector.tensor_tensor(mpart[:, 1, 0:NM], whole, mpart[:, 0, 0:NM],
                                                ALU.subtract).then_inc(m_cut, 1)
                        dve.wait_ge(m_turned, n + 1)
                        if steps is not first:
                            dve.wait_ge(m_sent, n * 32)
                        nc.vector.tensor_copy(mrow[:], ps[:, SIDE, :].bitcast(BF16)[:, 0:P]).then_inc(m_copied, 1)
                    elif what == "norm":
                        dve.wait_ge(o_turned, n * 2 + (k + 1))
                        if k == 1:
                            dve.wait_ge(normed, n * 2 + 1)
                        side = ps[:, SIDE, :].rearrange("p (a d) -> p a d", d=2 * HD)
                        nc.vector.reciprocal(rec[:, k, :], side[:, :, HD]).then_inc(o_rec, 1)
                        dve.wait_ge(o_rec, n * 2 + (k + 1))
                        nc.vector.tensor_tensor(
                            attn[:, one(n), k * CT:(k + 1) * CT, :].rearrange("p o t (h d) -> p (o t) h d", h=HG),
                            side[:, :, 0:HD].rearrange("p (t h) d -> p t h d", h=HG),
                            rec[:, k, :].rearrange("p (t h) -> p t h", h=HG).unsqueeze(3)
                            .to_broadcast((P, CT, HG, HD)), ALU.mult,
                        ).then_inc(normed, 1)
                    elif what in Preparation.STEPS:
                        prep.dve(dve, what, k)

            step(-1, -1, first)
            all_groups(dve, step)

        @block.scalar
        def _(act):
            def step(group, buf, steps):
                for what, k, later in steps:
                    n = group + later
                    if what == "exp":
                        half, kt = quads[k // HG]
                        lo, hi = columns_of(L, half, kt)
                        rows = key_tile(L, kt)[1]
                        q = k // HG
                        if k % HG == 0 and (q >= 2 or steps is not start):
                            act.wait_ge(values_done, n * NQ + (q - 1))
                        act.wait_ge(t_full, n * NX + (k + 1))
                        nc.scalar.activation(prob[0:rows, q % 2, k % HG, lo % CH:lo % CH + hi - lo],
                                             ps[0:rows, T_BANK + k % 2, lo % CH:lo % CH + hi - lo],
                                             ACT.Exp).then_inc(exp_done, 1)
                    elif what == "evict":
                        act.wait_ge(values_done, n * NQ + (last_quad[k] + 1))
                        if k == 1:
                            act.wait_ge(o_turned, n * 2 + 1)
                        nc.scalar.copy(ot[:], ps[:, O_BANK, :]).then_inc(evicted, 1)
                    elif what in Preparation.STEPS:
                        prep.act(act, what, k)

            all_groups(act, step)

        @block.tensor
        def _(pe):
            def score(k, par):
                h, qt, lo, hi = units[k]
                i0 = qt * P
                q = qop[0:RS, par, h, i0:i0 + P]

                def mm(a, b, lhs, rhs, start):
                    return nc.tensor.matmul(ps[:, S_BANK + k % S_SLOTS, a % CH:a % CH + b - a], lhs, rhs, start=start,
                                            stop=True, skip_group_check=True)

                if i == 0:
                    last = mm(lo, hi, q, kop[0:RS, par, h, lo:hi], True)
                    return mm(i0, i0 + P, identb[:], tri[:], False) if lo <= i0 < hi else last
                start = True
                for what, a, b, off in score_steps(qt):
                    if a // CH != lo // CH:
                        continue
                    if what == "band":
                        last = mm(a, b, identb[:], band[:, off:off + b - a], start)
                    elif what == "turn":
                        last = mm(a, b, turn[0:RS, h, i0:i0 + P], kop[0:RS, par, 0, a:b], start)
                    else:
                        last = mm(a, b, q, kop[0:RS, par, 0 if what == "left" else 1, a:b], start)
                    start = False
                return last

            def shifted(k, par):
                half, kt = quads[k // HG]
                h = k % HG
                lo, hi = columns_of(L, half, kt)
                j0, rows = key_tile(L, kt)
                q = qop[0:RA, par, h, :]

                def mm(a, b, lhs, rhs, start):
                    return nc.tensor.matmul(ps[0:rows, T_BANK + k % 2, a % CH:a % CH + b - a], lhs, rhs, start=start,
                                            stop=True, skip_group_check=True)

                if i == 0:
                    return mm(lo, hi, kop[0:RA, par, h, j0:j0 + P], q[:, lo:hi], True)
                start = True
                for v, a, b in ((1, 0, j0 + WIN), (2, j0 + WIN, j0 + 3 * WIN), (0, j0 + 3 * WIN, T)):
                    a, b = max(a, lo), min(b, hi)
                    if a < b:
                        last = mm(a, b, kop[0:RA, par, v, j0:j0 + rows], q[:, a:b], start)
                        start = False
                a, b = max(j0 - WIN, lo), min(j0 + P + WIN, hi)
                if a < b:
                    off = a - (j0 - WIN)
                    last = mm(a, b, identb[:, 0:rows], band[:, off:off + b - a], False)
                return last

            def values(qd, par):
                half, kt = quads[qd]
                lo, hi = columns_of(L, half, kt)
                vt_ = kt if key_tile(L, kt)[1] == P else TB
                opening = qd == 0 or quads[qd - 1][0] != half
                uniform = opening and i == 1 and half == 0
                if uniform:
                    for t in range(TB):
                        for h in range(HG):
                            nc.tensor.matmul(ps[32 * h:32 * h + 32, O_BANK, 0:GLOB], vst[:, par, t, 0, :],
                                             K.ones[:, 0:GLOB], start=(t == 0), stop=True, skip_group_check=True)
                for h in range(HG):
                    last = nc.tensor.matmul(ps[32 * h:32 * h + 32, O_BANK, lo % CH:lo % CH + hi - lo],
                                            vst[:, par, vt_, h % v_heads, :],
                                            prob[:, qd % 2, h, lo % CH:lo % CH + hi - lo],
                                            start=opening and not uniform, stop=True, skip_group_check=True)
                return last

            def step(group, buf, steps):
                for what, k, later in steps:
                    n = group + later
                    b = (buf + later) % BUFS
                    if what == "max":
                        if k == 0:
                            if steps is first:
                                pe.wait_ge(operands.const_rows[0], 16 * operands.consts * (BUFS - 1))
                            elif steps is steady:
                                pe.wait_ge(operands.const_rows[1], 16 * operands.consts)
                            pe.wait_ge(loaded[b], times_used(n, b) * (16 * operands.loads))
                            if i == 1:
                                pe.wait_ge(turn_loaded, n * 16 + 16)
                        if k % 2 == 0 and (steps is not first or k >= S_SLOTS):
                            pe.wait_ge(max_done, n * NU + (k + 2 - S_SLOTS))
                        score(k, b).then_inc(s_full, 1)
                    elif what == "rows":
                        pe.wait_ge(m_cut, n + 1)
                        if steps is not first:
                            pe.wait_ge(normed, n * 2 - 1)
                        nc.tensor.transpose(ps[:, SIDE, :].bitcast(BF16)[:, 0:P],
                                            mpart[:].rearrange("p k u -> p (k u)"), identb[:]).then_inc(m_turned, 1)
                    elif what == "exp":
                        if k == 0:
                            pe.wait_ge(m_sent, n * 32 + 32)
                            pe.wait_ge(v_staged, (n + 1) * (1 + i))
                        if k >= 2 or steps is not start:
                            pe.wait_ge(exp_done, n * NX + (k - 1))
                        shifted(k, b).then_inc(t_full, 1)
                    elif what == "values":
                        half = quads[k][0]
                        if k > 0 and half != quads[k - 1][0]:
                            pe.wait_ge(evicted, n * 2 + 1)
                        elif k == 0 and steps is not start:
                            pe.wait_ge(evicted, n * 2)
                        pe.wait_ge(exp_done, n * NX + HG * (k + 1))
                        if diagonal[k] is not None:
                            pe.wait_ge(masked, n * upto[-1] + upto[k])
                        values(k, b).then_inc(values_done, 1)
                    elif what == "norm":
                        pe.wait_ge(evicted, n * 2 + (k + 1))
                        if k == 1 and not (steps is final and later == 0):
                            pe.wait_ge(m_copied, n + 2)
                        elif k == 1 or steps is not start:
                            pe.wait_ge(normed, n * 2 + k)
                        else:
                            pe.wait_ge(m_copied, 1)
                        for j in range(CT):
                            last = nc.tensor.transpose(ps[:, SIDE, j * P:(j + 1) * P], ot[:, j * P:(j + 1) * P],
                                                       ident[:])
                        last.then_inc(o_turned, 1)
                    elif what in Preparation.STEPS:
                        prep.pe(pe, what, k)

            used = [0] * BUFS

            def times_used(n, b):
                return used[b]

            for b in range(BUFS):
                used[b] = 1
            step(-1, -1, first)
            step(0, 0, start)
            with pe.Fori(0, (N - 2) // BUFS) as turn_:
                for r in range(BUFS):
                    used[(r + 2) % BUFS] = turn_ + (1 + (r + 2) // BUFS)
                    step(turn_ * BUFS + (r + 1), (r + 1) % BUFS, steady)
            step(N - 1, (N - 1) % BUFS, final)


class Preparation:

    STEPS = ("gather", "turn_attn", "copy_attn", "project", "add", "inverse", "normalise", "turn_x", "high", "low")

    def __init__(self, nc, sem, sb, stack, K, L):
        tag = str(L.index)
        self.nc, self.K = nc, K
        self.wo_loaded = sem("wo_loaded" + tag)
        self.residual = sem("residual" + tag)
        self.normed = sem("normed" + tag)
        self.gathered = sem("gathered" + tag)
        self.a_full = sem("a_full" + tag)
        self.a_done = sem("a_done" + tag)
        self.y_full = sem("y_full" + tag)
        self.n_full = sem("n_full" + tag)
        self.n_hi = sem("n_hi" + tag)
        self.n_lo = sem("n_lo" + tag)
        self.gate_full = sem("gate_full" + tag)
        self.added = [sem(f"added{tag}{s}") for s in range(2)]
        self.stat = [sem(f"stat{tag}{s}") for s in range(2)]
        self.mean_done = [sem(f"mean_done{tag}{s}") for s in range(2)]
        self.eps_done = [sem(f"eps_done{tag}{s}") for s in range(2)]
        self.rstd = [sem(f"rstd{tag}{s}") for s in range(2)]
        self.normal = [sem(f"normal{tag}{s}") for s in range(2)]
        self.stats = sb(stack, "stats" + tag, [P, 2, NT, 6], F32)
        self.mv = sb(stack, "mv" + tag, [P, 2, NT, 2], F32)
        self.inv = sb(stack, "inv" + tag, [P, 2, 2, NT], F32)
        self.wo = sb(stack, "wo" + tag, [P, KD, D], F32)
        self.ag = K.staging[:, 0:CT * D].rearrange("p (t d) -> p t d", t=CT)
        self.at = K.staging[:, CT * D:].rearrange("p (k c) -> p k c", k=KD)
        self.xs = sb(stack, "xs" + tag, [P, 2, 2, KD, CH], F32R)

    def bank(self, c, k):
        return self.K.ps[:, (0, 2, 6, 6)[c] + k, :]

    def dve(self, dve, what, c):
        nc, K = self.nc, self.K
        if what == "gather":
            t0 = CT * c % TB
            g0 = (CT * c // TB) * NG
            dve.wait_ge(self.normed, 2 * (g0 + NG))
            if c >= 1:
                dve.wait_ge(self.a_full, KD * c)
            nc.vector.tensor_copy(self.ag.rearrange("p t (g d) -> p t g d", g=NG),
                                  K.attn[:, g0:g0 + NG, t0:t0 + CT, :].rearrange("p g t d -> p t g d")
                                  ).then_inc(self.gathered, 1)
        elif what == "copy_attn":
            if c >= 1:
                dve.wait_ge(self.y_full, 2 * c)
            for k in range(KD):
                dve.wait_ge(self.a_full, KD * c + k + 1)
                nc.vector.tensor_copy(self.at[:, k, :], self.bank(c, k)).then_inc(self.a_done, 1)
        elif what == "add":
            dve.wait_ge(self.residual, NT)
            for half in range(2):
                t0 = CT * c + 2 * half
                dst = K.x[:, t0:t0 + 2, :].rearrange("p t d -> p (t d)")
                dve.wait_ge(self.y_full, 2 * c + half + 1)
                nc.vector.tensor_tensor(dst, self.bank(c, half), dst, ALU.add).then_inc(self.added[0], 1)
            self.mean_and_variance(dve, c, 0)
        elif what == "normalise":
            self.normalise(dve, c, 0)
        elif what == "low":
            for k in range(KD):
                dve.wait_ge(self.n_hi, c * KD + k + 1)
                nc.vector.tensor_tensor(self.xs[:, c % 2, 1, k, :], self.bank(c, k),
                                        self.xs[:, c % 2, 0, k, :].bitcast(F32), ALU.subtract).then_inc(self.n_lo, 1)

    def mean_and_variance(self, dve, c, second):
        nc, x = self.nc, self.K.x
        for t in range(CT * c, CT * c + CT):
            dve.wait_ge(self.added[second], t // 2 + 1)
            nc.vector.bn_stats(self.stats[:, second, t, :], x[:, t, :]).then_inc(self.stat[second], 1)
        for t in range(CT * c, CT * c + CT):
            dve.wait_ge(self.stat[second], t + 1)
            nc.vector.bn_aggr(self.mv[:, second, t, :], self.stats[:, second, t, :]).then_inc(self.mean_done[second], 1)

    def normalise(self, dve, c, second):
        nc, x = self.nc, self.K.x
        dve.wait_ge(self.rstd[second], c + 1)
        for t in range(CT * c, CT * c + CT):
            nc.vector.tensor_scalar(x[:, t, :], x[:, t, :], self.mv[:, second, t, 0:1],
                                    self.inv[:, second, 1, t:t + 1], ALU.subtract, ALU.mult
                                    ).then_inc(self.normal[second], 1)

    def inverse(self, pool, c, second):
        nc = self.nc
        tiles = slice(CT * c, CT * c + CT)
        pool.wait_ge(self.mean_done[second], CT * (c + 1))
        nc.gpsimd.tensor_scalar(self.inv[:, second, 0, tiles], self.mv[:, second, tiles, 1], LN_EPS, 0.0, ALU.add,
                                ALU.add).then_inc(self.eps_done[second], 1)
        pool.wait_ge(self.eps_done[second], c + 1)
        nc.gpsimd.tensor_tensor(self.inv[:, second, 1, tiles], self.inv[:, second, 0, tiles], self.K.power[:],
                                ALU.pow).then_inc(self.rstd[second], 1)

    def act(self, act, what, c):
        nc = self.nc
        if what == "high":
            if c >= 2:
                act.wait_ge(self.gate_full, KE * (c - 1))
            for k in range(KD):
                act.wait_ge(self.n_full, c * KD + k + 1)
                nc.scalar.copy(self.xs[:, c % 2, 0, k, :], self.bank(c, k)).then_inc(self.n_hi, 1)

    def pe(self, pe, what, c):
        nc, K = self.nc, self.K
        if what == "turn_attn":
            pe.wait_ge(self.gathered, c + 1)
            if c == 3:
                pe.wait_ge(self.n_lo, KD * c)
            for k in range(KD):
                for j in range(CT):
                    last = nc.tensor.transpose(self.bank(c, k)[:, j * P:(j + 1) * P], self.ag[:, j, k * P:(k + 1) * P],
                                               K.ident[:])
                last.then_inc(self.a_full, 1)
        elif what == "project":
            if c == 0:
                pe.wait_ge(self.wo_loaded, 16)
            pe.wait_ge(self.a_done, KD * (c + 1))
            for half in range(2):
                for j in range(2 * half, 2 * half + 2):
                    for k in range(KD):
                        last = nc.tensor.matmul(self.bank(c, half)[:, (j % 2) * D:(j % 2 + 1) * D],
                                                self.at[:, k, j * P:(j + 1) * P], self.wo[:, k, :],
                                                start=(k == 0), stop=(k == KD - 1))
                last.then_inc(self.y_full, 1)
        elif what == "turn_x":
            pe.wait_ge(self.normal[0], CT * (c + 1))
            for k in range(KD):
                for j in range(CT):
                    last = nc.tensor.transpose(self.bank(c, k)[:, j * P:(j + 1) * P],
                                               K.x[:, CT * c + j, k * P:(k + 1) * P], K.ident[:])
                last.then_inc(self.n_full, 1)


def feed_forward(nc, sem, sb, K, L, dram, prep):
    i = L.index
    tag = str(i)
    ps, x = K.ps, K.x
    last_layer = i == 1
    up_full = sem("up_full" + tag)
    gate_full = prep.gate_full
    silu_done = sem("silu_done" + tag)
    hid = sem("hid" + tag)
    h_hi = sem("h_hi" + tag)
    h_lo = sem("h_lo" + tag)
    down_full = sem("down_full" + tag)
    stored = sem("stored" + tag)
    pairs = [(0, 0), (0, 1)] if i == 0 else [(0, 0), (0, 1), (1, 0)]
    between = {0: [("gather", 2)], 1: [("turn_attn", 2), ("copy_attn", 2)], 4: [("project", 2), ("add", 2)],
               5: [("inverse", 2), ("gather", 3)], 7: [("normalise", 2)], 9: [("turn_x", 2), ("high", 2), ("low", 2)],
               12: [("turn_attn", 3), ("copy_attn", 3)], 14: [("project", 3), ("add", 3)], 15: [("inverse", 3)],
               17: [("normalise", 3)], 19: [("turn_x", 3), ("high", 3), ("low", 3)]}
    with ExitStack() as st:
        hs = sb(st, "hs" + tag, [P, KE, 2, CH], F32R)
        sg = sb(st, "sg" + tag, [P, 2, CH], F32)
        hf = sb(st, "hf" + tag, [P, 2, CH], F32)
        w = K.wffn
        wup = [w[:, 0, s, :].rearrange("p (k n) -> p k n", k=KD) for s in range(1 + i)]
        wgate = [w[:, 1, s, :].rearrange("p (k n) -> p k n", k=KD) for s in range(1 + i)]
        wdown = [w[:, 2, s, :].rearrange("p (k n) -> p k n", k=KE) for s in range(1 + i)]
        out_dst = dram.out.rearrange("(t p) d -> p t d", p=P)
        block = st.enter_context(nc.Block())

        if last_layer:
            @block.sync
            def _(sp):
                for c in range(NC):
                    sp.wait_ge(prep.normal[1], CT * (c + 1))
                    sp.dma_start(out_dst[:, CT * c:CT * c + CT, :], x[:, CT * c:CT * c + CT, :]).then_inc(stored, 16)
                sp.wait_ge(stored, 16 * NC)

        @block.gpsimd
        def _(pool):
            for u in range(NC * KE):
                c, e = u // KE, u % KE
                pool.wait_ge(h_hi, u + 1)
                nc.gpsimd.tensor_tensor(hs[:, e, 1, :], hf[:, u % 2, :], hs[:, e, 0, :].bitcast(F32),
                                        ALU.subtract).then_inc(h_lo, 1)
                for what, k in between.get(u, ()):
                    if what == "inverse":
                        prep.inverse(pool, k, 0)
                if e == 3 and c >= 1:
                    prep.inverse(pool, c - 1, 1)
            prep.inverse(pool, NC - 1, 1)

        @block.scalar
        def _(act):
            def round_hidden(u):
                c, e = u // KE, u % KE
                act.wait_ge(hid, u + 1)
                if c >= 1 and e == 0:
                    act.wait_ge(down_full, 2 * c)
                nc.scalar.copy(hs[:, e, 0, :], hf[:, u % 2, :]).then_inc(h_hi, 1)

            for u in range(NC * KE):
                act.wait_ge(up_full, u + 1)
                if u >= 2:
                    act.wait_ge(hid, u - 1)
                nc.scalar.activation(sg[:, u % 2, :], ps[:, 2 * (u % 2), :], ACT.Silu,
                                     scale=K.scales[:, 0:1] if i == 0 else 1.0).then_inc(silu_done, 1)
                if u >= 1:
                    round_hidden(u - 1)
                for what, k in between.get(u, ()):
                    prep.act(act, what, k)
            round_hidden(NC * KE - 1)

        @block.vector
        def _(dve):
            def add_second(c):
                for half in range(2):
                    t0 = CT * c + 2 * half
                    dst = x[:, t0:t0 + 2, :].rearrange("p t d -> p (t d)")
                    dve.wait_ge(down_full, 2 * c + half + 1)
                    nc.vector.scalar_tensor_tensor(out=dst, in0=ps[:, 4 + half, :],
                                                   scalar=K.scales[:, 2:3] if i == 0 else 1.0, in1=dst,
                                                   op0=ALU.mult, op1=ALU.add).then_inc(prep.added[1], 1)
                prep.mean_and_variance(dve, c, 1)

            for u in range(NC * KE):
                c, e = u // KE, u % KE
                dve.wait_ge(gate_full, u + 1)
                dve.wait_ge(silu_done, u + 1)
                if u >= 2:
                    dve.wait_ge(h_lo, u - 1)
                nc.vector.scalar_tensor_tensor(out=hf[:, u % 2, :], in0=ps[:, 2 * (u % 2) + 1, :],
                                               scalar=K.scales[:, 1:2] if i == 0 else 1.0, in1=sg[:, u % 2, :],
                                               op0=ALU.mult, op1=ALU.mult).then_inc(hid, 1)
                for what, k in between.get(u, ()):
                    prep.dve(dve, what, k)
                if c >= 1 and e == 1:
                    add_second(c - 1)
                if c >= 1 and e == 5:
                    prep.normalise(dve, c - 1, 1)
            add_second(NC - 1)
            prep.normalise(dve, NC - 1, 1)

        @block.tensor
        def _(pe):
            def unit(u):
                c, e = u // KE, u % KE
                if e == 0 and c >= 2:
                    pe.wait_ge(prep.n_lo, KD * (c + 1))
                for which, weights, full in ((0, wup, up_full), (1, wgate, gate_full)):
                    if u >= 2:
                        pe.wait_ge(silu_done if which == 0 else hid, u - 1)
                    n = 0
                    for k in range(KD):
                        for a, b in pairs:
                            last = nc.tensor.matmul(ps[:, 2 * (u % 2) + which, :],
                                                    weights[a][:, k, e * P:(e + 1) * P],
                                                    prep.xs[:, c % 2, b, k, :],
                                                    start=(n == 0), stop=(n == KD * len(pairs) - 1))
                            n += 1
                    last.then_inc(full, 1)
                for what, k in between.get(u, ()):
                    prep.pe(pe, what, k)

            def down(c):
                pe.wait_ge(h_lo, KE * (c + 1))
                for half in range(2):
                    if c >= 1:
                        pe.wait_ge(prep.added[1], 2 * (c - 1) + half + 1)
                    for j in range(2 * half, 2 * half + 2):
                        n = 0
                        for e in range(KE):
                            for a, b in pairs:
                                last = nc.tensor.matmul(ps[:, 4 + half, (j % 2) * D:(j % 2 + 1) * D],
                                                        hs[:, e, b, j * P:(j + 1) * P], wdown[a][:, e, :],
                                                        start=(n == 0), stop=(n == KE * len(pairs) - 1))
                                n += 1
                    last.then_inc(down_full, 1)

            unit(0)
            unit(1)
            for c in range(NC):
                for u in range(c * KE + 2, min((c + 1) * KE + 2, NC * KE)):
                    unit(u)
                down(c)


def one(n):
    return slice(n, n + 1) if isinstance(n, int) else bass.ds(n, 1)


def build(nc, dram):
    layers = (Layer(0), Layer(1))
    dram.q_parts = [nc.dram_tensor(f"q_parts{i}", (PARTS, N, HD, HG * T), BF16, kind="Internal").ap()
                    for i in range(2)]
    dram.k_parts = [nc.dram_tensor(f"k_parts{i}", (PARTS, N, HD, (HG, 1)[i] * T), BF16, kind="Internal").ap()
                    for i in range(2)]
    with ExitStack() as top:
        def sb(stack, name, shape, dt):
            return stack.enter_context(nc.sbuf_tensor(name, shape, dt))

        def sem(name):
            return top.enter_context(nc.semaphore(name))

        K = Chip()
        K.ps = top.enter_context(nc.psum_tensor("ps", [P, 8, CH], F32))
        K.x = sb(top, "x", [P, NT, D], F32)
        K.ident = sb(top, "ident", [P, P], F32)
        K.identb = sb(top, "identb", [P, P], BF16)
        K.tri = sb(top, "tri", [P, P], BF16)
        K.band = sb(top, "band", [P, P + 2 * WIN], BF16)
        K.ones = sb(top, "ones", [P, P], F32)
        K.power = sb(top, "power", [P, CT], F32)
        K.scales = sb(top, "scales", [P, 3], F32)
        K.bias = sb(top, "bias", [P, 2, D], F32)
        for L in layers:
            with ExitStack() as layer:
                K.wffn = sb(layer, f"ffn_parts{L.index}", [P, 3, 1 + L.index, KD * E], F32R)
                K.attn = sb(layer, f"attn{L.index}", [P, N, TB, HG * HD], F32)
                K.staging = sb(layer, f"staging{L.index}", [P, KD * E], F32)
                prep = Preparation(nc, sem, sb, layer, K, L)
                with ExitStack() as values:
                    K.v_all = sb(values, f"v_all{L.index}", [P, N, TB, L.kv_width // NG], F32)
                    K.qop = sb(values, f"qop{L.index}", [P, BUFS, HG, T], BF16)
                    K.kop = sb(values, f"kop{L.index}", [P, BUFS, L.key_sets, T], BF16)
                    K.operands = Operands(nc, sem, K, L, dram)
                    project(nc, sem, sb, K, L, dram, prep)
                    attend(nc, sem, sb, K, L, dram, prep)
                feed_forward(nc, sem, sb, K, L, dram, prep)


def bf16_bits(a):
    u = np.ascontiguousarray(a, np.float32).view(np.uint32)
    return ((u + 0x7FFF + ((u >> 16) & 1)) >> 16).astype(np.uint16)


def three_parts(a):
    parts = []
    for _ in range(PARTS):
        p = (bf16_bits(a).astype(np.uint32) << 16).view(np.float32)
        parts.append(p)
        a = a - p
    return parts


def constants():
    r = np.arange(P)
    tri = np.where(r[None, :] > r[:, None], -1e30, 0.0)
    c = np.arange(P + 2 * WIN)
    band = np.where(np.abs(c[None, :] - WIN - r[:, None]) <= WIN, -1e9, 0.0)
    pos = np.arange(T)
    high, low, unit = (pos // P * P).astype(np.float32), (pos % P).astype(np.float32), np.ones(T, np.float32)
    left = np.stack([high] * 3 + [low] * 3 + [unit] * 3)
    mixed = np.where(((pos - GLOB) // GLOB) % 2 == 0, 1.0, -1.0).astype(np.float32)
    kpos = np.stack([left, -left, left * mixed], axis=1)
    slopes = np.float32(2.0 ** (-(2.0 ** -(np.log2(H) - 3.0)))) ** np.arange(1, H + 1, dtype=np.float32)
    s = three_parts(slopes)
    g = three_parts(-(slopes[:, None] * pos[None, :].astype(np.float32)))
    qpos = np.stack([np.broadcast_to(a[:, None], (H, T)) for a in (*s, *s)] + g).astype(np.float32)
    late = (pos % P >= P // 2).astype(np.float32)

    def by_group(a):
        a = a.reshape(NPOS, NG, HG, T).transpose(1, 0, 2, 3)
        return np.concatenate([a] * B)

    return {
        "ident": np.eye(P, dtype=np.float32), "identb": bf16_bits(np.eye(P)),
        "tri": bf16_bits(tri), "band": bf16_bits(band), "kpos": bf16_bits(kpos),
        "qpos": bf16_bits(by_group(qpos)), "qturn": bf16_bits(by_group(2.0 * qpos * late)),
    }


def kernel(**inputs):
    import concourse.bacc as bacc
    from concourse.bass_utils import run_bass_kernel_spmd as run

    a = {k: np.asarray(v) for k, v in inputs.items()}
    def head_minor(w):
        blocks = [w[:, j:j + D].reshape(D, NG, HG, HD).transpose(0, 1, 3, 2).reshape(D, D)
                  for j in range(0, min(w.shape[1], 2 * D), D)]
        return np.concatenate(blocks + [w[:, 2 * D:]], axis=1)

    arrays = {
        "x": a["L0_attn_x"].reshape(TOK, D),
        "w_qkv0": head_minor(a["L0_attn_w_qkv"]), "w_out0": a["L0_attn_w_out"], "b_out0": a["L0_attn_b_out"].reshape(1, D),
        "up0": a["L0_ffn_W_up"].T, "gate0": a["L0_ffn_W_gate"].T, "down0": a["L0_ffn_W_down"].T,
        "w_q1": head_minor(a["L1_attn_Wq"]), "w_kv1": a["L1_attn_Wkv"], "w_out1": a["L1_attn_Wo"],
        "b_out1": a["L1_attn_bo"].reshape(1, D),
        "gate1": a["L1_ffn_w_gate"].T, "up1": a["L1_ffn_w_up"].T, "down1": a["L1_ffn_w_down"].T,
        **constants(),
    }
    arrays = {k: np.ascontiguousarray(v) for k, v in arrays.items()}
    nc = bacc.Bacc("TRN2", target_bir_lowering=False, num_devices=1)
    t = {k: nc.dram_tensor("in_" + k, v.shape, mybir.dt.from_np(v.dtype), kind="ExternalInput").ap()
         for k, v in arrays.items()}
    t = {k: v.bitcast(BF16) if v.dtype == mybir.dt.uint16 else v for k, v in t.items()}
    out = nc.dram_tensor("out", (TOK, D), F32, kind="ExternalOutput").ap()
    dram = Dram()
    dram.x, dram.out = t["x"], out
    dram.ident, dram.identb, dram.tri, dram.band = t["ident"], t["identb"], t["tri"], t["band"]
    dram.kpos, dram.qpos, dram.qturn = t["kpos"], t["qpos"], t["qturn"]
    dram.wq, dram.wkv = (t["w_qkv0"], t["w_q1"]), t["w_kv1"]
    dram.wo, dram.bias = (t["w_out0"], t["w_out1"]), (t["b_out0"], t["b_out1"])
    dram.ffn = ((t["up0"], t["gate0"], t["down0"]), (t["gate1"], t["up1"], t["down1"]))
    build(nc, dram)
    r = run(nc, [{"in_" + k: v for k, v in arrays.items()}], core_ids=[0])
    return r.results[0]["out"].reshape(B, T, D)
```
